# Optimizing a Trainium2 kernel written in Bass

```python
import numpy as np
import jax
import jax.numpy as jnp

def _softmax(x, axis=-1):
    return jax.nn.softmax(x, axis=axis)

def _gelu(x):
    return jax.nn.gelu(x, approximate=True)

def _silu(x):
    return jax.nn.silu(x)

def _sigmoid(x):
    return jax.nn.sigmoid(x)

def _layernorm(x, axis=-1, eps=1e-05):
    m = jnp.mean(x, axis=axis, keepdims=True)
    v = jnp.var(x, axis=axis, keepdims=True)
    return (x - m) / jnp.sqrt(v + eps)

def _scatter_add(tgt, idx, src, axis=0):
    return tgt.at[idx].add(src)

def _segment_sum(src, seg, n):
    return jax.ops.segment_sum(src, seg, n)
kernel_name = 'mk_gnn_resnorm_d1_gnn_r64_4ea468'

def setup_inputs(seed: int=0):
    np.random.seed(seed)
    _w = jnp.asarray

    def _rec_inputs():
        import jax
        import jax.numpy as jnp
        _gk = jax.random.key(seed)
        x = -8.776e-05 + 1 * jax.random.normal(jax.random.fold_in(_gk, 1), (100000, 256), jnp.float32)
        src = jax.random.randint(jax.random.fold_in(_gk, 2), (25000,), 0, 100000, jnp.int32)
        dst = jax.random.randint(jax.random.fold_in(_gk, 3), (25000,), 0, 100000, jnp.int32)
        _o = jnp.argsort(dst, stable=True)
        src = src[_o]
        dst = dst[_o]
        return (x, src, dst)
    x, src, dst = _rec_inputs()

    def _L0_gnn_setup():
        import jax, jax.numpy as jnp
        import numpy as np
        N_NODES = 20000
        N_EDGES = 5000
        D = 256
        N_LAYERS = 3
        BN_EPS = 1e-05
        key = jax.random.key(seed)
        ks = jax.random.split(key, 5)
        x = jax.random.normal(ks[0], (N_NODES, D), dtype=jnp.float32)
        src = jax.random.randint(ks[1], (N_EDGES,), 0, N_NODES)
        dst = jax.random.randint(ks[2], (N_EDGES,), 0, N_NODES)
        scale = 1.0 / np.sqrt(D)
        thetas = jax.random.normal(ks[3], (N_LAYERS, D, D), dtype=jnp.float32) * scale
        phis = jax.random.normal(ks[4], (N_LAYERS, D, D), dtype=jnp.float32) * scale
        gammas = jnp.ones((N_LAYERS, D), dtype=jnp.float32)
        betas = jnp.zeros((N_LAYERS, D), dtype=jnp.float32)
        return {'x': x, 'src': src, 'dst': dst, 'thetas': thetas, 'phis': phis, 'gammas': gammas, 'betas': betas}
    _L0_gnn_all = _L0_gnn_setup()
    _L0_gnn_in = {k: v for k, v in _L0_gnn_all.items() if k in ('thetas', 'phis', 'gammas', 'betas')}
    del _L0_gnn_all
    return {'x': x, 'src': src, 'dst': dst, 'L0_gnn_thetas': _L0_gnn_in['thetas'], 'L0_gnn_phis': _L0_gnn_in['phis'], 'L0_gnn_gammas': _L0_gnn_in['gammas'], 'L0_gnn_betas': _L0_gnn_in['betas']}

def reference(x, src, dst, L0_gnn_thetas, L0_gnn_phis, L0_gnn_gammas, L0_gnn_betas):
    import jax
    import jax.numpy as jnp

    def _L0_gnn_ref(x, src, dst, thetas, phis, gammas, betas):
        import jax, jax.numpy as jnp
        import numpy as np
        N_NODES = 20000
        N_EDGES = 5000
        D = 256
        N_LAYERS = 3
        BN_EPS = 1e-05
        N = x.shape[0]
        for l in range(thetas.shape[0]):
            xi = x[src]
            xj = x[dst]
            e = jax.nn.relu((xj - xi) @ thetas[l].T + xi @ phis[l].T)
            agg = jax.ops.segment_max(e, src, num_segments=N)
            agg = jnp.where(agg < -1e+30, 0.0, agg)
            mu = agg.mean(axis=0)
            var = agg.var(axis=0)
            x = jax.nn.relu((agg - mu) * jax.lax.rsqrt(var + BN_EPS) * gammas[l] + betas[l])
        return x
    x = _layernorm(x + _L0_gnn_ref(x, src, dst, L0_gnn_thetas, L0_gnn_phis, L0_gnn_gammas, L0_gnn_betas), axis=-1)
    return x

_drawn_inputs = setup_inputs


def setup_inputs(seed=0):
    import zlib

    import numpy as np

    out = dict(_drawn_inputs(seed))
    spreads = {'L0_gnn_gammas': (1.0, 0.2), 'L0_gnn_betas': (0.0, 0.1)}
    factors = {}
    for name, (base, spread) in spreads.items():
        noise = np.random.default_rng([zlib.crc32(name.encode()), seed]).standard_normal(out[name].shape)
        drawn = base * np.exp(spread * noise) if base else spread * noise
        out[name] = jnp.asarray(drawn.astype(out[name].dtype))
    for name, factor in factors.items():
        out[name] = (out[name] * factor).astype(out[name].dtype)
    return out
```

```python
import concourse.bass as bass
from concourse import mybir
from contextlib import ExitStack


def loop(engine, count, step, peeled=1):
    head = min(peeled, count - 1)
    for i in range(head):
        step(i, i == 0, False)
    if count - 1 > head:
        with engine.Fori(head, count - 1) as i:
            step(i, False, False)
    step(count - 1, count == 1, True)


class Chain:

    def __init__(self, engine, sem):
        self.engine, self.sem, self.base, self.count, self.per_step = engine, sem, 0, 0, None

    def step(self, i):
        if self.per_step is None and self.count:
            self.per_step = self.count
        self.base = 0 if self.per_step is None else i * self.per_step
        self.count = 0

    def mark(self, instruction):
        self.count += 1
        instruction.then_inc(self.sem, 1)

    def after(self):
        self.engine.wait_ge(self.sem, self.base + self.count)


def gnn_program(nc, x, src, dst, thetas, phis, gammas, betas, out):
    f32, i32 = mybir.dt.float32, mybir.dt.int32
    f16, bf16 = mybir.dt.float16, mybir.dt.bfloat16
    ALU = mybir.AluOpType
    ACT = mybir.ActivationFunctionType
    AX_X = mybir.AxisListType.X

    P = 128
    N, D = x.shape
    E = src.shape[0]
    LAYERS = thetas.shape[0]
    KD = D // P
    EPS = 1e-5
    EP = -(-E // 1024) * 1024
    NT = EP // P
    TC = NT // 2
    G = 4
    GE = G * P
    STEPS = EP // (2 * GE)
    NG = 2 * STEPS
    LOW = 512
    LOW_BITS = 9
    HC = -(-(N + 1) // (2 * LOW))
    HIGHS = 2 * HC
    PAD_KEY = N
    ABSENT = EP
    START_PENALTY = -2e38
    END_PENALTY = -1e30
    SKIP = float(1 << 20)
    assert HC <= P and TC <= P and D == KD * P and N < (1 << 20)

    R = 10
    BLOCK_ROWS = P * R
    BLOCK_STEPS = N // (2 * BLOCK_ROWS)
    REST = N - 2 * BLOCK_STEPS * BLOCK_ROWS
    RR = max((r for r in range(1, R + 1) if REST % r == 0 and REST // r <= P), default=0)
    assert REST == 0 or RR

    src_row = nc.dram_tensor("src_row", (EP,), f32).ap()
    high_row = nc.dram_tensor("high_row", (EP,), f32).ap()
    position_table = nc.dram_tensor("position_table", (HIGHS * LOW, 1), i32).ap()
    sorted_meta = nc.dram_tensor("sorted_meta", (EP, 4), i32).ap()
    sorted_row = nc.dram_tensor("sorted_row", (EP + 2,), f32).ap()
    start_row = nc.dram_tensor("start_row", (EP,), bf16).ap()
    end_row = nc.dram_tensor("end_row", (EP,), bf16).ap()
    agg_rows = [nc.dram_tensor(f"agg_rows{l}", (EP + 1, D), f32).ap() for l in range(LAYERS)]
    agg_cols = [nc.dram_tensor(f"agg_cols{l}", (NG, P, KD * GE), f32).ap() for l in range(LAYERS - 1)]

    whole = ExitStack()
    with whole:
        def sb(name, shape, dt, ctx=whole):
            return ctx.enter_context(nc.sbuf_tensor(name, shape, dt))

        def pb(name, shape, dt, ctx=whole):
            return ctx.enter_context(nc.psum_tensor(name, shape, dt))

        ident = sb("ident", [P, P], f32)
        ones = sb("ones", [P, P], f32)
        ones_bf = sb("ones_bf", [1, P], bf16)
        gat_src = sb("gat_src", [P, NT], i32)
        gat_dst = sb("gat_dst", [P, NT], i32)
        gat_pos = sb("gat_pos", [P, NT], i32)
        put_src = sb("put_src", [P, NT], i32)
        bn_a = sb("bn_a", [P, KD], f32)
        bn_b = sb("bn_b", [P, KD], f32)
        gam = sb("gam", [P, KD, LAYERS], f32)
        bet = sb("bet", [P, KD, LAYERS], f32)

        sorting = ExitStack()
        with sorting:
            src_col = sb("src_col", [P, NT], f32, sorting)
            low_col = sb("low_col", [P, NT], f32, sorting)
            high_col = sb("high_col", [P, NT], f32, sorting)
            meta = sb("meta", [P, NT, 2], i32, sorting)
            iota_low = sb("iota_low", [P, LOW], f16, sorting)
            iota_high = sb("iota_high", [P, HIGHS], f16, sorting)
            iota_part = sb("iota_part", [P, 2], f32, sorting)
            earlier = sb("earlier", [P, GE], f16, sorting)
            below = sb("below", [P, P], f32, sorting)
            first_pos = sb("first_pos", [HC, 2, LOW], f32, sorting)
            counts = [pb(f"counts{c}", [HC, LOW], f32, sorting) for c in range(2)]

            with ExitStack() as ctx:
                raw = sb("raw", [TC, 2, 2, P], i32, ctx)
                rawf = sb("rawf", [TC, 2, 2, P], f32, ctx)
                high_i = sb("high_i", [TC, 2, P], i32, ctx)
                high_f = sb("high_f", [TC, 2, P], f32, ctx)
                col_i = sb("col_i", [P, 3, NT], i32, ctx)
                zrow = sb("zrow", [1, D], f32, ctx)
                tp = [pb(f"tp{s}", [P, NT], f32, ctx) for s in range(2)]
                s_fill = ctx.enter_context(nc.semaphore("s_fill"))
                s_raw = ctx.enter_context(nc.semaphore("s_raw"))
                s_const = ctx.enter_context(nc.semaphore("s_const"))
                s_pool = ctx.enter_context(nc.semaphore("s_pool"))
                s_rawf = ctx.enter_context(nc.semaphore("s_rawf"))
                s_tp = ctx.enter_context(nc.semaphore("s_tp"))
                s_dve = ctx.enter_context(nc.semaphore("s_dve"))
                s_out = ctx.enter_context(nc.semaphore("s_out"))
                s_high = ctx.enter_context(nc.semaphore("s_high"))
                loads = [0]
                with nc.Block() as block:
                    @block.sync
                    def _(sp):
                        sp.wait_ge(s_fill, 1)
                        for which, edges in enumerate((src, dst)):
                            for c in range(2):
                                full = max(min(E // P - c * TC, TC), 0)
                                if full:
                                    sp.dma_start(raw[0:full, which, c, :], edges[c * TC * P:(c * TC + full) * P]
                                                 .rearrange("(t p) -> t p", p=P)).then_inc(s_raw, 16)
                                    loads[0] += 16
                                if full < TC and E % P and full == E // P - c * TC:
                                    sp.dma_start(raw[full:full + 1, which, c, 0:E % P],
                                                 edges[E - E % P:E].unsqueeze(0)).then_inc(s_raw, 16)
                                    loads[0] += 16
                        with nc.allow_non_contiguous_dma(reason="small, once"):
                            for k in range(KD):
                                for l in range(LAYERS):
                                    sp.dma_start(gam[:, k, l:l + 1], gammas[l, k * P:(k + 1) * P].unsqueeze(1)).then_inc(s_out, 16)
                                    sp.dma_start(bet[:, k, l:l + 1], betas[l, k * P:(k + 1) * P].unsqueeze(1)).then_inc(s_out, 16)
                        sp.wait_ge(s_rawf, 1)
                        sp.dma_start(src_row.rearrange("(c t p) -> t c p", c=2, p=P), rawf[:, 0, :, :]).then_inc(s_out, 16)
                        sp.wait_ge(s_high, 1)
                        sp.dma_start(high_row.rearrange("(c t p) -> t c p", c=2, p=P), high_f[:, :, :]).then_inc(s_out, 16)
                        sp.wait_ge(s_const, 1)
                        for l in range(LAYERS - 1):
                            sp.dma_start(agg_rows[l][ABSENT:ABSENT + 1, :], zrow[:, :]).then_inc(s_out, 16)
                        sp.wait_ge(s_out, 16 * (2 * KD * LAYERS + 2 + LAYERS - 1))

                    @block.gpsimd
                    def _(pool):
                        chain = Chain(pool, s_pool)
                        nc.gpsimd.memset(raw[:, 1, :, :], 0)
                        nc.gpsimd.memset(raw[:, 0, :, :], PAD_KEY).then_inc(s_fill, 1)
                        nc.gpsimd.memset(zrow[:], 0.0)
                        nc.gpsimd.memset(ones_bf[:], 1.0)
                        nc.gpsimd.memset(ones[:], 1.0)
                        nc.gpsimd.memset(ident[:], 0.0)
                        nc.gpsimd.memset(below[:], 1.0)
                        chain.mark(nc.gpsimd.memset(earlier[:], 1.0))
                        chain.after()
                        nc.gpsimd.affine_select(out=ident[:], in_=ident[:], compare_op=ALU.not_equal, fill=1.0, base=0,
                                                pattern=[[1, P]], channel_multiplier=-1)
                        nc.gpsimd.affine_select(out=below[:], in_=below[:], compare_op=ALU.is_gt, fill=0.0, base=0,
                                                pattern=[[1, P]], channel_multiplier=-1)
                        nc.gpsimd.affine_select(out=earlier[:, GE - P:GE], in_=earlier[:, GE - P:GE], compare_op=ALU.is_gt,
                                                fill=0.0, base=0, pattern=[[-1, P]], channel_multiplier=1)
                        nc.gpsimd.iota(iota_low[:], [[1, LOW]], base=0, channel_multiplier=0, allow_small_or_imprecise_dtypes=True)
                        nc.gpsimd.iota(iota_high[:], [[1, HIGHS]], base=0, channel_multiplier=0, allow_small_or_imprecise_dtypes=True)
                        nc.gpsimd.iota(iota_part[:], [[HC, 2]], base=0, channel_multiplier=1,
                                       allow_small_or_imprecise_dtypes=True).then_inc(s_const, 1)

                    @block.vector
                    def _(dve):
                        chain = Chain(dve, s_dve)
                        dve.wait_ge(s_raw, loads[0])
                        nc.vector.tensor_copy(rawf[:], raw[:]).then_inc(s_rawf, 1)
                        chain.mark(nc.vector.tensor_single_scalar(high_i[:], raw[:, 0, :, :], LOW_BITS, ALU.logical_shift_right))
                        chain.after()
                        nc.vector.tensor_copy(high_f[:], high_i[:]).then_inc(s_high, 1)
                        dve.wait_ge(s_tp, 1)
                        nc.vector.tensor_copy(src_col[:], tp[0][:, :])
                        nc.vector.tensor_copy(meta[:, :, 0], tp[0][:, :])
                        nc.vector.tensor_copy(meta[:, :, 1], tp[1][:, :])
                        chain.mark(nc.vector.tensor_copy(col_i[:, 0, :], tp[0][:, :]))
                        chain.after()
                        nc.vector.tensor_single_scalar(col_i[:, 1, :], col_i[:, 0, :], LOW_BITS, ALU.logical_shift_right)
                        chain.mark(nc.vector.tensor_single_scalar(col_i[:, 2, :], col_i[:, 0, :], LOW - 1, ALU.bitwise_and))
                        chain.after()
                        nc.vector.tensor_copy(high_col[:], col_i[:, 1, :])
                        nc.vector.tensor_copy(low_col[:], col_i[:, 2, :])

                    @block.tensor
                    def _(pe):
                        pe.wait_ge(s_const, 1)
                        pe.wait_ge(s_rawf, 1)
                        for which in range(2):
                            for c in range(2):
                                last = nc.tensor.transpose(tp[which][:, c * TC:(c + 1) * TC], rawf[:, which, c, :], ident[0:TC, 0:TC])
                        last.then_inc(s_tp, 1)

            with ExitStack() as ctx:
                hot_high = sb("hot_high", [P, 2, G, HIGHS], f16, ctx)
                hot_low = sb("hot_low", [P, 2, G, LOW], f16, ctx)
                incl = sb("incl", [HC, 2, LOW], f32, ctx)
                cnt = sb("cnt", [HC, 2, LOW], f32, ctx)
                ones_low = sb("ones_low", [HC, LOW], f32, ctx)
                base = sb("base", [HC, 2], f32, ctx)
                table = sb("table", [HC, 2, LOW], i32, ctx)
                base_ps = pb("base_ps", [HC, 2], f32, ctx)
                hot_ready = ctx.enter_context(nc.semaphore("hot_ready"))
                hot_used = ctx.enter_context(nc.semaphore("hot_used"))
                s_tot = ctx.enter_context(nc.semaphore("s_tot"))
                s_base = ctx.enter_context(nc.semaphore("s_base"))
                s_dve = ctx.enter_context(nc.semaphore("s_dve2"))
                s_table = ctx.enter_context(nc.semaphore("s_table"))
                s_stored = ctx.enter_context(nc.semaphore("s_stored"))
                with nc.Block() as block:
                    @block.vector
                    def _(dve):
                        def step(i, first, last):
                            for b in range(2):
                                g = 2 * i + b
                                if not first:
                                    dve.wait_ge(hot_used, g - 1)
                                for j in range(G):
                                    t = G * g + j
                                    nc.vector.tensor_scalar(hot_high[:, b, j, :], iota_high[:], high_col[:, bass.ds(t, 1)], None, ALU.is_equal)
                                    ins = nc.vector.tensor_scalar(hot_low[:, b, j, :], iota_low[:], low_col[:, bass.ds(t, 1)], None, ALU.is_equal)
                                ins.then_inc(hot_ready, 1)
                        loop(dve, STEPS, step)

                        chain = Chain(dve, s_dve)
                        nc.vector.memset(ones_low[:], 1.0)
                        dve.wait_ge(hot_used, NG)
                        for c in range(2):
                            chain.mark(nc.vector.tensor_copy(cnt[:, c, :], counts[c][:, :]))
                        chain.after()
                        for c in range(2):
                            ins = nc.vector.tensor_tensor_scan(incl[:, c, :], ones_low[:], cnt[:, c, :], 0.0, ALU.mult, ALU.add)
                        ins.then_inc(s_tot, 1)
                        dve.wait_ge(s_base, 1)
                        chain.mark(nc.vector.tensor_copy(base[:], base_ps[:]))
                        chain.after()
                        for c in range(2):
                            chain.mark(nc.vector.tensor_scalar(incl[:, c, :], incl[:, c, :], base[:, c:c + 1], None, ALU.add))
                        chain.after()
                        chain.mark(nc.vector.tensor_tensor(first_pos[:], incl[:], cnt[:], ALU.subtract))
                        chain.after()
                        chain.mark(nc.vector.tensor_scalar(incl[:], incl[:], -1.0 - ABSENT, None, ALU.add))
                        chain.after()
                        chain.mark(nc.vector.scalar_tensor_tensor(cnt[:], cnt[:], 0.0, incl[:], ALU.is_gt, ALU.mult))
                        chain.after()
                        nc.vector.tensor_scalar(table[:], cnt[:], float(ABSENT), None, ALU.add).then_inc(s_table, 1)

                    @block.tensor
                    def _(pe):
                        def step(i, first, last):
                            for b in range(2):
                                g = 2 * i + b
                                pe.wait_ge(hot_ready, g + 1)
                                for j in range(G):
                                    for c in range(2):
                                        ins = nc.tensor.matmul(counts[c][:, :], hot_high[:, b, j, c * HC:(c + 1) * HC], hot_low[:, b, j, :],
                                                               start=(first and b == 0 and j == 0), stop=(last and b == 1 and j == G - 1),
                                                               skip_group_check=True)
                                ins.then_inc(hot_used, 1)
                        loop(pe, STEPS, step)
                        pe.wait_ge(s_tot, 1)
                        nc.tensor.matmul(base_ps[:, 0:1], below[0:HC, 0:HC], incl[:, 0, LOW - 1:LOW], start=True, stop=True)
                        nc.tensor.matmul(base_ps[:, 1:2], below[0:HC, 0:HC], incl[:, 1, LOW - 1:LOW], start=True, stop=False)
                        nc.tensor.matmul(base_ps[:, 1:2], ones[0:HC, 0:HC], incl[:, 0, LOW - 1:LOW], start=False, stop=True).then_inc(s_base, 1)

                    @block.sync
                    def _(sp):
                        sp.wait_ge(s_table, 1)
                        sp.dma_start(position_table.rearrange("(c h l) o -> h c (l o)", c=2, l=LOW), table[:]).then_inc(s_stored, 16)
                        sp.wait_ge(s_stored, 16)

            with ExitStack() as ctx:
                hot_high = sb("hot_high2", [P, 2, G, HIGHS], f16, ctx)
                hot_low = sb("hot_low2", [P, 2, G, LOW], f16, ctx)
                hot_rows = sb("hot_rows", [HC, 2, 2, GE], f16, ctx)
                keys = sb("keys", [P, 2, GE], f32, ctx)
                highs = sb("highs", [HC, 2, GE], f32, ctx)
                c_hi = sb("c_hi", [HC, 2, 2, LOW], f16, ctx)
                c_lo = sb("c_lo", [HC, 2, 2, LOW], f16, ctx)
                junk = sb("junk", [P, G, LOW], f16, ctx)
                junk2 = sb("junk2", [P, G, LOW], f16, ctx)
                same = sb("same", [P, 2, G], f32, ctx)
                before = sb("before", [P, 2, G], f32, ctx)
                pos = sb("pos", [P, 2, G], i32, ctx)
                row = sb("row", [P, 2, G, 4], i32, ctx)
                idx = sb("idx", [P, 2, G], i32, ctx)
                found = [pb(f"found{j}", [P, LOW], f32, ctx) for j in range(G)]
                names = ("hi_ready", "lo_ready", "rows_ready", "hot_ready2", "found_ready", "found_used", "next_ready",
                         "row_ready", "pos_ready", "keys_used", "s_dve3", "seeded")
                (hi_ready, lo_ready, rows_ready, hot_ready, found_ready, found_used, next_ready,
                 row_ready, pos_ready, keys_used, s_dve, seeded) = [ctx.enter_context(nc.semaphore(n)) for n in names]
                keys_in = [ctx.enter_context(nc.semaphore(f"keys_in{b}")) for b in range(2)]
                looked_up = [ctx.enter_context(nc.semaphore(f"looked_up{b}")) for b in range(2)]
                scattered = [ctx.enter_context(nc.semaphore(f"scattered{b}")) for b in range(2)]
                with nc.Block() as block:
                    @block.sync
                    def _(sp):
                        def step(i, first, last):
                            for b in range(2):
                                g = 2 * i + b
                                if not first:
                                    sp.wait_ge(keys_used, g - 1)
                                sp.dma_start(keys[:, b, :], src_row[bass.ds(g * GE, GE)].partition_broadcast(P)).then_inc(keys_in[b], 16)
                                sp.dma_start(highs[:, b, :], high_row[bass.ds(g * GE, GE)].partition_broadcast(HC)).then_inc(keys_in[b], 16)
                        loop(sp, STEPS, step)

                    @block.scalar
                    def _(act):
                        def step(i, first, last):
                            for b in range(2):
                                g = 2 * i + b
                                act.wait_ge(next_ready, g + 1)
                                if not first:
                                    act.wait_ge(found_ready, G * (g - 1))
                                for c in range(2):
                                    ins = nc.scalar.copy(c_hi[:, b, c, :], counts[c][:, :])
                                ins.then_inc(hi_ready, 1)
                        loop(act, STEPS, step)

                    @block.tensor
                    def _(pe):
                        for c in range(2):
                            ins = nc.tensor.matmul(counts[c][:, :], ident[0:HC, 0:HC], first_pos[:, c, :], start=True, stop=False,
                                                   skip_group_check=True)
                        ins.then_inc(next_ready, 1)

                        def step(i, first, last):
                            for b in range(2):
                                g = 2 * i + b
                                pe.wait_ge(rows_ready, g + 1)
                                pe.wait_ge(hi_ready, g + 1)
                                pe.wait_ge(lo_ready, g + 1)
                                for j in range(G):
                                    if not (first and b == 0):
                                        pe.wait_ge(found_used, G * (g - 1) + j + 1)
                                    n = 0
                                    for c in range(2):
                                        for part in (c_hi, c_lo):
                                            ins = nc.tensor.matmul(found[j][:, :], hot_rows[:, b, c, j * P:(j + 1) * P], part[:, b, c, :],
                                                                   start=(n == 0), stop=(n == 3))
                                            n += 1
                                    ins.then_inc(found_ready, 1)
                                pe.wait_ge(hot_ready, g + 1)
                                for j in range(G):
                                    for c in range(2):
                                        ins = nc.tensor.matmul(counts[c][:, :], hot_high[:, b, j, c * HC:(c + 1) * HC], hot_low[:, b, j, :],
                                                               start=False, stop=(last and b == 1 and j == G - 1), skip_group_check=True)
                                ins.then_inc(next_ready, 1)
                        loop(pe, STEPS, step)

                    @block.vector
                    def _(dve):
                        chain = Chain(dve, s_dve)

                        def step(i, first, last):
                            chain.step(i)
                            for b in range(2):
                                g = 2 * i + b
                                dve.wait_ge(keys_in[b], 32 * i + 32)
                                if not first:
                                    dve.wait_ge(found_ready, G * (g - 1))
                                    dve.wait_ge(next_ready, g)
                                for c in range(2):
                                    ins = nc.vector.tensor_scalar(hot_rows[:, b, c, :], highs[:, b, :], iota_part[0:HC, c:c + 1], None, ALU.is_equal)
                                ins.then_inc(rows_ready, 1)
                                dve.wait_ge(hi_ready, g + 1)
                                for c in range(2):
                                    ins = nc.vector.tensor_tensor(c_lo[:, b, c, :], counts[c][:, :], c_hi[:, b, c, :], ALU.subtract)
                                ins.then_inc(lo_ready, 1)
                                for j in range(G):
                                    t = G * g + j
                                    nc.vector.tensor_scalar(hot_high[:, b, j, :], iota_high[:], high_col[:, bass.ds(t, 1)], None, ALU.is_equal)
                                    ins = nc.vector.tensor_scalar(hot_low[:, b, j, :], iota_low[:], low_col[:, bass.ds(t, 1)], None, ALU.is_equal)
                                ins.then_inc(hot_ready, 1)
                                if not first:
                                    dve.wait_ge(scattered[b], 64 * i)
                                nc.vector.tensor_copy(row[:, b, :, 0:2], meta[:, bass.ds(G * g, G), :])
                                nc.vector.memset(row[:, b, :, 3], 0)
                                nc.vector.tensor_copy(idx[:, b, :], meta[:, bass.ds(G * g, G), 1]).then_inc(row_ready, 1)
                                for j in range(G):
                                    t = G * g + j
                                    wide = (j + 1) * P
                                    ins = nc.vector.scalar_tensor_tensor(junk[:, j, 0:wide], keys[:, b, 0:wide], src_col[:, bass.ds(t, 1)],
                                                                         earlier[:, GE - wide:GE], ALU.is_equal, ALU.mult,
                                                                         accum_out=same[:, b, j:j + 1])
                                ins.then_inc(keys_used, 1)
                                dve.wait_ge(keys_used, g + 1)
                                for j in range(G):
                                    dve.wait_ge(found_ready, G * g + j + 1)
                                    ins = nc.vector.scalar_tensor_tensor(junk2[:, j, :], found[j][:, :], 1.0, hot_low[:, b, j, :], ALU.mult, ALU.mult,
                                                                         accum_out=before[:, b, j:j + 1])
                                    ins.then_inc(found_used, 1)
                                dve.wait_ge(found_used, G * g + G)
                                nc.vector.tensor_tensor(pos[:, b, :], same[:, b, :], before[:, b, :], ALU.add).then_inc(pos_ready, 1)
                        loop(dve, STEPS, step)

                    @block.gpsimd
                    def _(pool):
                        def step(i, first, last):
                            for b in range(2):
                                g = 2 * i + b
                                pool.wait_ge(row_ready, g + 1)
                                pool.nop(nofuse=True)
                                for j in range(G):
                                    nc.gpsimd.indirect_dma_start(row[:, b, j, 2:3], None, position_table[:, :],
                                                                 bass.IndirectOffsetOnAxis(ap=idx[:, b, j:j + 1], axis=0)).then_inc(looked_up[b], 16)
                                pool.wait_ge(looked_up[b], 64 * i + 64)
                                pool.wait_ge(pos_ready, g + 1)
                                pool.nop(nofuse=True)
                                for j in range(G):
                                    nc.gpsimd.indirect_dma_start(sorted_meta[:, :], bass.IndirectOffsetOnAxis(ap=pos[:, b, j:j + 1], axis=0),
                                                                 row[:, b, j, :], None).then_inc(scattered[b], 16)
                        loop(pool, STEPS, step)
                        for b in range(2):
                            pool.wait_ge(scattered[b], 64 * STEPS)
                            pool.nop(nofuse=True)

        mask = sb("mask", [P, EP], bf16)

        with ExitStack() as ctx:
            sm = sb("sm", [TC, 2, P, 4], i32, ctx)
            here = sb("here", [TC, 2, P], f32, ctx)
            prev = sb("prev", [TC, 2, P], f32, ctx)
            nxt = sb("nxt", [TC, 2, P], f32, ctx)
            cols = sb("cols", [TC, 4, 2, P], f32, ctx)
            flag = sb("flag", [TC, 2, P], f32, ctx)
            pen = sb("pen", [TC, 2, 2, P], bf16, ctx)
            edge = sb("edge", [1, 2], f32, ctx)
            tp = [pb(f"tq{s}", [P, NT], f32, ctx) for s in range(4)]
            names = ("m_in", "here_ready", "edge_ready", "row_out", "shift_in", "pens_ready", "pens_out", "cols_ready", "tp_ready", "s_dve4", "mask_in", "edge_out")
            (m_in, here_ready, edge_ready, row_out, shift_in, pens_ready, pens_out, cols_ready, tp_ready, s_dve, mask_in, edge_out) = [
                ctx.enter_context(nc.semaphore(n)) for n in names]
            with nc.Block() as block:
                @block.sync
                def _(sp):
                    sp.dma_start(sm[:].rearrange("t c p m -> t c (p m)"), sorted_meta.rearrange("(c t p) m -> t c (p m)", c=2, p=P)).then_inc(m_in, 16)
                    sp.wait_ge(edge_ready, 1)
                    sp.dma_start(sorted_row[0:1].unsqueeze(0), edge[:, 0:1]).then_inc(row_out, 16)
                    sp.dma_start(sorted_row[EP + 1:EP + 2].unsqueeze(0), edge[:, 1:2]).then_inc(row_out, 16)
                    sp.wait_ge(here_ready, 1)
                    sp.dma_start(sorted_row[1:EP + 1].rearrange("(c t p) -> t c p", c=2, p=P), here[:]).then_inc(row_out, 16)
                    sp.wait_ge(row_out, 48)
                    sp.dma_start(prev[:], sorted_row[0:EP].rearrange("(c t p) -> t c p", c=2, p=P)).then_inc(shift_in, 16)
                    sp.dma_start(nxt[:], sorted_row[2:EP + 2].rearrange("(c t p) -> t c p", c=2, p=P)).then_inc(shift_in, 16)
                    sp.wait_ge(pens_ready, 1)
                    sp.dma_start(start_row.rearrange("(c t p) -> t c p", c=2, p=P), pen[:, 0, :, :]).then_inc(pens_out, 16)
                    sp.dma_start(end_row.rearrange("(c t p) -> t c p", c=2, p=P), pen[:, 1, :, :]).then_inc(pens_out, 16)
                    sp.wait_ge(pens_out, 32)
                    sp.dma_start(mask[:], start_row.partition_broadcast(P)).then_inc(mask_in, 16)
                    sp.wait_ge(mask_in, 16)

                @block.vector
                def _(dve):
                    chain = Chain(dve, s_dve)
                    nc.vector.memset(edge[:, 0:1], -1.0)
                    nc.vector.memset(edge[:, 1:2], float(N + 1)).then_inc(edge_ready, 1)
                    dve.wait_ge(m_in, 16)
                    nc.vector.tensor_copy(here[:], sm[:, :, :, 0]).then_inc(here_ready, 1)
                    nc.vector.tensor_copy(cols[:, 1, :, :], sm[:, :, :, 1])
                    nc.vector.tensor_copy(cols[:, 2, :, :], sm[:, :, :, 2])
                    dve.wait_ge(here_ready, 1)
                    nc.vector.tensor_scalar(cols[:, 0, :, :], here[:], float(N - 1), None, ALU.min)
                    dve.wait_ge(shift_in, 32)
                    chain.mark(nc.vector.tensor_tensor(prev[:], here[:], prev[:], ALU.not_equal))
                    chain.mark(nc.vector.tensor_tensor(nxt[:], here[:], nxt[:], ALU.is_equal))
                    chain.after()
                    nc.vector.tensor_scalar(pen[:, 0, :, :], prev[:], START_PENALTY, None, ALU.mult)
                    chain.mark(nc.vector.scalar_tensor_tensor(flag[:], here[:], float(N), nxt[:], ALU.is_ge, ALU.max))
                    chain.after()
                    nc.vector.tensor_scalar(pen[:, 1, :, :], flag[:], END_PENALTY, None, ALU.mult).then_inc(pens_ready, 1)
                    nc.vector.scalar_tensor_tensor(cols[:, 3, :, :], flag[:], SKIP, here[:], ALU.mult, ALU.add).then_inc(cols_ready, 1)
                    dve.wait_ge(tp_ready, 1)
                    for s, to in enumerate((gat_src, gat_dst, gat_pos, put_src)):
                        nc.vector.tensor_copy(to[:], tp[s][:, :])

                @block.tensor
                def _(pe):
                    pe.wait_ge(cols_ready, 1)
                    for s in range(4):
                        for c in range(2):
                            ins = nc.tensor.transpose(tp[s][:, c * TC:(c + 1) * TC], cols[:, s, c, :], ident[0:TC, 0:TC])
                    ins.then_inc(tp_ready, 1)

        for layer in range(LAYERS):
            one = layer == 0
            more = layer < LAYERS - 1
            with ExitStack() as ctx:
                L = str(layer)
                w_raw = sb("w_raw" + L, [P, 2, KD, D], f32, ctx)
                w_neigh = sb("w_neigh" + L, [P, KD, D], f32, ctx)
                w_self = sb("w_self" + L, [P, KD, D], f32, ctx)
                fresh = sb("fresh" + L, [P, 2, G, D], f32, ctx)
                own = sb("own" + L, [P, 2, G, D], f32, ctx)
                idx = sb("idx" + L, [P, 2, 2, G], i32, ctx)
                pen = sb("pen" + L, [1, 2, GE], bf16, ctx)
                xj = sb("xj" + L, [P, 2, KD, GE], f32, ctx)
                xi = sb("xi" + L, [P, 2, KD, GE], f32, ctx)
                top = sb("top" + L, [P, 2, KD, GE], f32, ctx)
                summ = sb("summ" + L, [P, 2, KD, GE], f32, ctx)
                agg = sb("agg" + L, [P, 2, KD, GE], f32, ctx)
                sq = sb("sq" + L, [P, GE], f32, ctx)
                rows = sb("rows" + L, [P, 2, G, D], f32, ctx)
                sums = sb("sums" + L, [P, 2, KD, NG], f32, ctx)
                stat = sb("stat" + L, [P, 6, KD], f32, ctx)
                xt_ps = pb("xt_ps" + L, [P, KD, GE], f32, ctx)
                y_ps = [pb(f"y_ps{m}" + L, [P, GE], f32, ctx) for m in range(KD)]
                z_ps = [pb(f"z_ps{m}" + L, [P, GE], f32, ctx) for m in range(KD)]
                row_ps = pb("row_ps" + L, [P, G, D], f32, ctx)
                names = ("w_in", "w_t", "w_ev", "idx_ready", "j_turned", "i_turned", "j_ready", "i_ready", "yz_ready", "sum_ready",
                         "agg_ready", "sq_ready", "row_turned", "row_ready", "s_dve", "s_act", "sd_ready", "var_ready")
                (w_in, w_t, w_ev, idx_ready, j_turned, i_turned, j_ready, i_ready, yz_ready, sum_ready,
                 agg_ready, sq_ready, row_turned, row_ready, s_dve, s_act, sd_ready, var_ready) = [
                    ctx.enter_context(nc.semaphore(n + L)) for n in names]
                j_in, i_in, pen_in, agg_out, row_out = [[ctx.enter_context(nc.semaphore(f"{n}{b}_{L}")) for b in range(2)]
                                                        for n in ("j_in", "i_in", "pen_in", "agg_out", "row_out")]
                with nc.Block() as block:
                    @block.gpsimd
                    def _(pool):
                        def step(i, first, last):
                            for b in range(2):
                                g = 2 * i + b
                                if not first:
                                    pool.wait_ge(j_turned, g - 1)
                                    if one:
                                        pool.wait_ge(i_turned, g - 1)
                                    pool.nop(nofuse=True)
                                cols = gat_dst if one else gat_pos
                                ins = nc.gpsimd.tensor_copy(idx[:, b, 0, :], cols[:, bass.ds(G * g, G)])
                                if one:
                                    ins = nc.gpsimd.tensor_copy(idx[:, b, 1, :], gat_src[:, bass.ds(G * g, G)])
                                ins.then_inc(idx_ready, 1)
                                pool.wait_ge(idx_ready, g + 1)
                                pool.nop(nofuse=True)
                                from_ = x if one else agg_rows[layer - 1]
                                for j in range(G):
                                    nc.gpsimd.indirect_dma_start(fresh[:, b, j, :], None, from_[:, :],
                                                                 bass.IndirectOffsetOnAxis(ap=idx[:, b, 0, j:j + 1], axis=0)).then_inc(j_in[b], 16)
                                if one:
                                    for j in range(G):
                                        nc.gpsimd.indirect_dma_start(own[:, b, j, :], None, x[:, :],
                                                                     bass.IndirectOffsetOnAxis(ap=idx[:, b, 1, j:j + 1], axis=0)).then_inc(i_in[b], 16)
                        loop(pool, STEPS, step)

                    @block.sync
                    def _(sp):
                        sp.dma_start(w_raw[:, 0, :, :], thetas[layer].rearrange("(m o) i -> o m i", o=P)).then_inc(w_in, 16)
                        sp.dma_start(w_raw[:, 1, :, :], phis[layer].rearrange("(m o) i -> o m i", o=P)).then_inc(w_in, 16)

                        def load(g, b):
                            sp.dma_start(pen[:, b, :], end_row[bass.ds(g * GE, GE)].unsqueeze(0)).then_inc(pen_in[b], 16)
                            if not one:
                                sp.dma_start(own[:, b, :, :].rearrange("p a d -> p (a d)"),
                                             agg_cols[layer - 1][bass.ds(g, 1), :, :].rearrange("a p f -> p (a f)")).then_inc(i_in[b], 16)

                        for b in range(2):
                            load(b, b)

                        def store_rows(g, b):
                            sp.wait_ge(row_ready, g + 1)
                            sp.dma_start(agg_rows[layer][bass.ds(g * GE, GE), :].rearrange("(a p) d -> p a d", p=P), rows[:, b, :, :]).then_inc(row_out[b], 16)

                        def step(i, first, last):
                            for b in range(2):
                                g = 2 * i + b
                                if not last:
                                    sp.wait_ge(yz_ready, 2 * g + 2)
                                    if not one:
                                        sp.nop(nofuse=True)
                                        sp.wait_ge(i_ready, g + 1)
                                    load(g + 2, b)
                                if more:
                                    sp.wait_ge(agg_ready, 2 * g + 2)
                                    sp.dma_start(agg_cols[layer][bass.ds(g, 1), :, :].rearrange("a p f -> p (a f)"),
                                                 agg[:, b, :, :].rearrange("p k f -> p (k f)")).then_inc(agg_out[b], 16)
                                if not (first and b == 0):
                                    store_rows(g - 1, 1 - b)
                        loop(sp, STEPS, step)
                        store_rows(NG - 1, 1)
                        for b in range(2):
                            sp.wait_ge(row_out[b], 16 * STEPS)
                            if more:
                                sp.wait_ge(agg_out[b], 16 * STEPS)

                    @block.tensor
                    def _(pe):
                        pe.wait_ge(w_in, 32)
                        for s in range(2):
                            if s == 1:
                                pe.wait_ge(w_ev, 1)
                            for m in range(KD):
                                for k in range(KD):
                                    ins = nc.tensor.transpose(xt_ps[:, k, m * P:(m + 1) * P], w_raw[:, s, m, k * P:(k + 1) * P], ident[:])
                            ins.then_inc(w_t, 1)

                        def turn(rows_, b, signal):
                            for j in range(G):
                                for k in range(KD):
                                    ins = nc.tensor.transpose(xt_ps[:, k, j * P:(j + 1) * P], rows_[:, b, j, k * P:(k + 1) * P], ident[:])
                            ins.then_inc(signal, 1)

                        def turn_j(g, i, b, start):
                            pe.wait_ge(j_in[b], 64 * i + 64)
                            if start:
                                pe.wait_ge(w_ev, 2)
                            else:
                                pe.wait_ge(i_ready if one else j_ready, g)
                            turn(fresh, b, j_turned)

                        def turn_i(g, i, b):
                            pe.wait_ge(i_in[b], 64 * i + 64)
                            pe.wait_ge(j_ready, g + 1)
                            turn(own, b, i_turned)

                        def products(g, i, b, start):
                            pe.wait_ge(j_ready, g + 1)
                            pe.wait_ge(i_ready, g + 1)
                            pe.wait_ge(pen_in[b], 16 * i + 16)
                            for m in range(KD):
                                if not start:
                                    pe.wait_ge(sum_ready, 2 * g - 1 + m)
                                for k in range(KD):
                                    nc.tensor.matmul(y_ps[m][:, :], w_neigh[:, k, m * P:(m + 1) * P], xj[:, b, k, :], start=(k == 0), stop=(k == KD - 1))
                                for k in range(KD):
                                    nc.tensor.matmul(z_ps[m][:, :], w_self[:, k, m * P:(m + 1) * P], xi[:, b, k, :], start=(k == 0), stop=False)
                                nc.tensor.matmul(z_ps[m][:, :], ones_bf[:, :], pen[:, b, :], start=False, stop=True).then_inc(yz_ready, 1)

                        def turn_back(g, b, start):
                            pe.wait_ge(agg_ready, 2 * g + 2)
                            if not start:
                                pe.wait_ge(row_ready, g)
                            for j in range(G):
                                for k in range(KD):
                                    ins = nc.tensor.transpose(row_ps[:, j, k * P:(k + 1) * P], agg[:, b, k, j * P:(j + 1) * P], ident[:])
                            ins.then_inc(row_turned, 1)

                        turn_j(0, 0, 0, True)
                        if one:
                            turn_i(0, 0, 0)

                        def step(i, first, last):
                            for b in range(2):
                                g = 2 * i + b
                                start = first and b == 0
                                products(g, i, b, start)
                                ahead = not (last and b == 1)
                                if ahead:
                                    turn_j(g + 1, i + b, 1 - b, False)
                                if not start:
                                    turn_back(g - 1, 1 - b, first and b == 1)
                                if ahead and one:
                                    turn_i(g + 1, i + b, 1 - b)
                        loop(pe, STEPS, step)
                        turn_back(NG - 1, 1, False)

                    @block.scalar
                    def _(act):
                        def columns(g, i, b, start2):
                            act.wait_ge(j_turned, g + 1)
                            if not start2:
                                act.wait_ge(yz_ready, 2 * g - 2)
                            for k in range(KD):
                                if one:
                                    ins = nc.scalar.copy(xj[:, b, k, :], xt_ps[:, k, :])
                                else:
                                    ins = nc.scalar.activation(xj[:, b, k, :], xt_ps[:, k, :], ACT.Relu, bias=bn_b[:, k:k + 1], scale=bn_a[:, k:k + 1])
                            ins.then_inc(j_ready, 1)
                            if one:
                                act.wait_ge(i_turned, g + 1)
                            else:
                                act.wait_ge(i_in[b], 16 * i + 16)
                            own_k = own[:, b, :, :].rearrange("p a d -> p (a d)")
                            for k in range(KD):
                                if one:
                                    ins = nc.scalar.copy(xi[:, b, k, :], xt_ps[:, k, :])
                                else:
                                    ins = nc.scalar.activation(xi[:, b, k, :], own_k[:, k * GE:(k + 1) * GE], ACT.Relu, bias=bn_b[:, k:k + 1], scale=bn_a[:, k:k + 1])
                            ins.then_inc(i_ready, 1)

                        columns(0, 0, 0, True)

                        def step(i, first, last):
                            for b in range(2):
                                g = 2 * i + b
                                if not (last and b == 1):
                                    columns(g + 1, i + b, 1 - b, first and b == 0)
                                for m in range(KD):
                                    act.wait_ge(sum_ready, 2 * g + m + 1)
                                    if not first and m == 0:
                                        act.wait_ge(row_turned, g - 1)
                                        if more:
                                            act.wait_ge(agg_out[b], 16 * i)
                                    nc.scalar.activation(agg[:, b, m, :], summ[:, b, m, :], ACT.Relu,
                                                         accum_out=sums[:, 0, m, bass.ds(g, 1)]).then_inc(agg_ready, 1)
                                    act.wait_ge(agg_ready, 2 * g + m + 1)
                                    nc.scalar.activation(sq[:], agg[:, b, m, :], ACT.Square,
                                                         accum_out=sums[:, 1, m, bass.ds(g, 1)]).then_inc(sq_ready, 1)
                        loop(act, STEPS, step)
                        act.wait_ge(var_ready, 1)
                        nc.scalar.activation(stat[:, 3, :], stat[:, 2, :], ACT.Sqrt).then_inc(sd_ready, 1)

                    @block.vector
                    def _(dve):
                        dve.wait_ge(w_t, 1)
                        nc.vector.tensor_copy(w_neigh[:], xt_ps[:, :, 0:D]).then_inc(w_ev, 1)
                        for b in range(2):
                            for m in range(KD):
                                nc.vector.memset(top[:, b, m, GE - 1:GE], 0.0)
                        dve.wait_ge(w_t, 2)
                        dve.wait_ge(w_ev, 1)
                        nc.vector.tensor_tensor(w_self[:], xt_ps[:, :, 0:D], w_neigh[:], ALU.subtract).then_inc(w_ev, 1)
                        dve.wait_ge(w_ev, 2)
                        chain = Chain(dve, s_dve)

                        def step(i, first, last):
                            chain.step(i)
                            for b in range(2):
                                g = 2 * i + b
                                for m in range(KD):
                                    dve.wait_ge(yz_ready, 2 * g + m + 1)
                                    chain.mark(nc.vector.tensor_tensor_scan(top[:, b, m, :], mask[:, bass.ds(g * GE, GE)], y_ps[m][:, :],
                                                                            top[:, 1 - b, m, GE - 1:GE], ALU.add, ALU.max))
                                    if not first:
                                        dve.wait_ge(agg_ready, 2 * g - 3 + m)
                                    chain.after()
                                    nc.vector.tensor_tensor(summ[:, b, m, :], z_ps[m][:, :], top[:, b, m, :], ALU.add).then_inc(sum_ready, 1)
                                if b == 1:
                                    dve.wait_ge(row_turned, g)
                                    if not first:
                                        dve.wait_ge(row_out[0], 16 * i)
                                    nc.vector.tensor_copy(rows[:, 0, :, :], row_ps[:, :, :]).then_inc(row_ready, 1)
                                elif not first:
                                    dve.wait_ge(row_turned, g)
                                    if not (isinstance(i, int) and i < 2):
                                        dve.wait_ge(row_out[1], 16 * (i - 1))
                                    nc.vector.tensor_copy(rows[:, 1, :, :], row_ps[:, :, :]).then_inc(row_ready, 1)
                        loop(dve, STEPS, step, peeled=2)
                        dve.wait_ge(row_turned, NG)
                        if STEPS > 1:
                            dve.wait_ge(row_out[1], 16 * (STEPS - 1))
                        nc.vector.tensor_copy(rows[:, 1, :, :], row_ps[:, :, :]).then_inc(row_ready, 1)

                        dve.wait_ge(sq_ready, 2 * NG)
                        base_count = chain.base + chain.count
                        n = [base_count]

                        def link(ins):
                            n[0] += 1
                            ins.then_inc(s_dve, 1)
                            dve.wait_ge(s_dve, n[0])

                        for s in range(2):
                            link(nc.vector.tensor_reduce(stat[:, s, :], sums[:, s, :, :], AX_X, ALU.add))
                        link(nc.vector.tensor_scalar(stat[:, 0:2, :], stat[:, 0:2, :], 1.0 / N, None, ALU.mult))
                        link(nc.vector.tensor_tensor(stat[:, 2, :], stat[:, 0, :], stat[:, 0, :], ALU.mult))
                        link(nc.vector.tensor_tensor(stat[:, 2, :], stat[:, 1, :], stat[:, 2, :], ALU.subtract))
                        nc.vector.tensor_scalar(stat[:, 2, :], stat[:, 2, :], 0.0, EPS, ALU.max, ALU.add).then_inc(var_ready, 1)
                        dve.wait_ge(sd_ready, 1)
                        link(nc.vector.reciprocal(stat[:, 4, :], stat[:, 3, :]))
                        link(nc.vector.tensor_tensor(bn_a[:], stat[:, 4, :], gam[:, :, layer], ALU.mult))
                        link(nc.vector.tensor_tensor(stat[:, 5, :], stat[:, 0, :], bn_a[:], ALU.mult))
                        nc.vector.tensor_tensor(bn_b[:], bet[:, :, layer], stat[:, 5, :], ALU.subtract)

        a_row = sb("a_row", [P, D], f32)
        b_row = sb("b_row", [P, D], f32)
        base_row = sb("base_row", [P, D], f32)
        with ExitStack() as ctx:
            spread = sb("spread", [P, 2, KD, P], f32, ctx)
            row_ps = pb("rowc_ps", [P, 2, D], f32, ctx)
            SL = 3
            xin = sb("xin", [P, SL, R, D], f32, ctx)
            xout = sb("xout", [P, 2, R, D], f32, ctx)
            bstats = sb("bstats", [P, R, 6], f32, ctx)
            aggr = sb("aggr", [P, 2, R, 2], f32, ctx)
            sd = sb("sd", [P, 2, R], f32, ctx)
            rstd = sb("rstd", [P, 2, R], f32, ctx)
            shift = sb("shift", [P, 2, R], f32, ctx)
            names = ("spread_ready", "row_ready", "s_dve", "aggr_ready", "sd_ready", "norm_ready", "y_ready", "rows_set")
            (spread_ready, row_ready, s_dve, aggr_ready, sd_ready, norm_ready, y_ready, rows_set) = [
                ctx.enter_context(nc.semaphore(n + "_f")) for n in names]
            in_ready, out_done = [[ctx.enter_context(nc.semaphore(f"{n}{b}")) for b in range(2)] for n in ("in_ready", "out_done")]
            x_blocks = x[0:N - REST, :].rearrange("(n p r) d -> n p (r d)", p=P, r=R)
            out_blocks = out[0:N - REST, :].rearrange("(n p r) d -> n p (r d)", p=P, r=R)
            QP = REST // RR if REST else 0
            with nc.Block() as block:
                @block.sync
                def _(sp):
                    def load(n, b):
                        sp.dma_start(xin[:, b, :, :].rearrange("p r d -> p (r d)"), x_blocks[bass.ds(n, 1), :, :].rearrange("a p f -> p (a f)")).then_inc(in_ready[b], 16)
                    for b in range(2):
                        load(b, b)

                    def step(i, first, last):
                        for b in range(2):
                            n = 2 * i + b
                            if not last:
                                sp.wait_ge(y_ready, n + 1)
                                load(n + 2, b)
                    loop(sp, BLOCK_STEPS, step)
                    if REST:
                        sp.wait_ge(y_ready, 2 * BLOCK_STEPS - 1)
                        sp.dma_start(xin[0:QP, 0, 0:RR, :].rearrange("p r d -> p (r d)"),
                                     x[N - REST:N, :].rearrange("(p r) d -> p (r d)", r=RR)).then_inc(in_ready[0], 16)

                @block.tensor
                def _(pe):
                    pe.wait_ge(spread_ready, 1)
                    for s in range(2):
                        for k in range(KD):
                            ins = nc.tensor.matmul(row_ps[:, s, k * P:(k + 1) * P], spread[:, s, k, :], ident[:], start=True, stop=True)
                    ins.then_inc(row_ready, 1)

                @block.vector
                def _(dve):
                    for s, col in enumerate((bn_a, bn_b)):
                        for k in range(KD):
                            ins = nc.vector.tensor_scalar(spread[:, s, k, :], ones[:], col[:, k:k + 1], None, ALU.mult)
                    ins.then_inc(spread_ready, 1)
                    dve.wait_ge(row_ready, 1)
                    nc.vector.tensor_copy(a_row[:], row_ps[:, 0, :])
                    nc.vector.tensor_copy(b_row[:], row_ps[:, 1, :])
                    nc.vector.tensor_scalar(base_row[:], row_ps[:, 1, :], 0.0, None, ALU.max).then_inc(rows_set, 1)
                    dve.wait_ge(rows_set, 1)
                    chain = Chain(dve, s_dve)

                    def block_of(n, i, b, np_, r_, free):
                        dve.wait_ge(in_ready[b], 16 * i + 16)
                        v = xin[0:np_, b, 0:r_, :]
                        chain.mark(nc.vector.tensor_tensor(v, v, base_row[0:np_, :].unsqueeze(1).broadcast_to([np_, r_, D]), ALU.add))
                        chain.after()
                        for r in range(r_):
                            ins = nc.vector.bn_stats(bstats[0:np_, r, :], xin[0:np_, b, r, :])
                        chain.mark(ins)
                        chain.after()
                        if not free:
                            dve.wait_ge(y_ready, n - 1)
                        dve.nop(nofuse=True)
                        for r in range(r_):
                            ins = nc.vector.bn_aggr(aggr[0:np_, b, r, :], bstats[0:np_, r, :])
                        chain.mark(ins)
                        chain.after()
                        nc.vector.tensor_scalar(sd[0:np_, b, 0:r_], aggr[0:np_, b, 0:r_, 1], EPS, None, ALU.add).then_inc(aggr_ready, 1)
                        dve.wait_ge(sd_ready, n + 1)
                        chain.mark(nc.vector.reciprocal(rstd[0:np_, b, 0:r_], sd[0:np_, b, 0:r_]))
                        chain.after()
                        nc.vector.scalar_tensor_tensor(shift[0:np_, b, 0:r_], aggr[0:np_, b, 0:r_, 0], -1.0, rstd[0:np_, b, 0:r_],
                                                       ALU.mult, ALU.mult).then_inc(norm_ready, 1)

                    def step(i, first, last):
                        chain.step(i)
                        for b in range(2):
                            block_of(2 * i + b, i, b, P, R, first)
                    loop(dve, BLOCK_STEPS, step)
                    if REST:
                        chain.step(BLOCK_STEPS)
                        block_of(2 * BLOCK_STEPS, BLOCK_STEPS, 0, QP, RR, False)

                @block.scalar
                def _(act):
                    def block_of(n, i, b, np_, r_, free, store):
                        act.wait_ge(aggr_ready, n + 1)
                        nc.scalar.activation(sd[0:np_, b, 0:r_], sd[0:np_, b, 0:r_], ACT.Sqrt).then_inc(sd_ready, 1)
                        act.wait_ge(norm_ready, n + 1)
                        if not free:
                            act.wait_ge(out_done[b], 16 * i)
                        for r in range(r_):
                            ins = nc.scalar.activation(xout[0:np_, b, r, :], xin[0:np_, b, r, :], ACT.Identity,
                                                       bias=shift[0:np_, b, r:r + 1], scale=rstd[0:np_, b, r:r + 1])
                        ins.then_inc(y_ready, 1)
                        act.wait_ge(y_ready, n + 1)
                        store()

                    def step(i, first, last):
                        for b in range(2):
                            n = 2 * i + b
                            block_of(n, i, b, P, R, first, lambda: act.dma_start(
                                out_blocks[bass.ds(n, 1), :, :].rearrange("a p f -> p (a f)"),
                                xout[:, b, :, :].rearrange("p r d -> p (r d)")).then_inc(out_done[b], 16))
                    loop(act, BLOCK_STEPS, step)
                    if REST:
                        block_of(2 * BLOCK_STEPS, BLOCK_STEPS, 0, QP, RR, False, lambda: act.dma_start(
                            out[N - REST:N, :].rearrange("(p r) d -> p (r d)", r=RR),
                            xout[0:QP, 0, 0:RR, :].rearrange("p r d -> p (r d)")).then_inc(out_done[0], 16))
                    act.wait_ge(out_done[0], 16 * (BLOCK_STEPS + (1 if REST else 0)))
                    act.wait_ge(out_done[1], 16 * BLOCK_STEPS)

        with ExitStack() as ctx:
            xs = sb("xs", [P, 2, G, D], f32, ctx)
            ag = sb("ag", [P, 2, G, D], f32, ctx)
            yo = sb("yo", [P, 2, G, D], f32, ctx)
            idx = sb("idxf", [P, 2, 2, G], i32, ctx)
            bstats = sb("bstats2", [P, G, 6], f32, ctx)
            aggr = sb("aggr2", [P, 2, G, 2], f32, ctx)
            sd = sb("sd2", [P, 2, G], f32, ctx)
            rstd = sb("rstd2", [P, 2, G], f32, ctx)
            shift = sb("shift2", [P, 2, G], f32, ctx)
            names = ("idx_ready", "s_dve", "aggr_ready", "sd_ready", "norm_ready", "y_ready")
            (idx_ready, s_dve, aggr_ready, sd_ready, norm_ready, y_ready) = [ctx.enter_context(nc.semaphore(n + "_g")) for n in names]
            x_in, a_in, put = [[ctx.enter_context(nc.semaphore(f"{n}{b}_g")) for b in range(2)] for n in ("x_in", "a_in", "put")]
            with nc.Block() as block:
                @block.sync
                def _(sp):
                    def step(i, first, last):
                        for b in range(2):
                            g = 2 * i + b
                            if not first:
                                sp.wait_ge(y_ready, g - 1)
                            sp.dma_start(ag[:, b, :, :], agg_rows[LAYERS - 1][bass.ds(g * GE, GE), :].rearrange("(a p) d -> p a d", p=P)).then_inc(a_in[b], 16)
                    loop(sp, STEPS, step)

                @block.gpsimd
                def _(pool):
                    def fetch(g, i, b, free):
                        if not free:
                            pool.wait_ge(y_ready, g - 1)
                            pool.wait_ge(put[b], 64 * i)
                            pool.nop(nofuse=True)
                        nc.gpsimd.tensor_copy(idx[:, b, 0, :], gat_src[:, bass.ds(G * g, G)])
                        nc.gpsimd.tensor_copy(idx[:, b, 1, :], put_src[:, bass.ds(G * g, G)]).then_inc(idx_ready, 1)
                        pool.wait_ge(idx_ready, g + 1)
                        pool.nop(nofuse=True)
                        for j in range(G):
                            nc.gpsimd.indirect_dma_start(xs[:, b, j, :], None, x[:, :],
                                                         bass.IndirectOffsetOnAxis(ap=idx[:, b, 0, j:j + 1], axis=0)).then_inc(x_in[b], 16)
                    fetch(0, 0, 0, True)

                    def step(i, first, last):
                        for b in range(2):
                            g = 2 * i + b
                            if not (last and b == 1):
                                fetch(g + 1, i + b, 1 - b, first and b == 0)
                            pool.wait_ge(y_ready, g + 1)
                            pool.nop(nofuse=True)
                            for j in range(G):
                                nc.gpsimd.indirect_dma_start(out[:, :], bass.IndirectOffsetOnAxis(ap=idx[:, b, 1, j:j + 1], axis=0),
                                                             yo[:, b, j, :], None, bounds_check=N - 1, oob_is_err=False).then_inc(put[b], 16)
                    loop(pool, STEPS, step)
                    for b in range(2):
                        pool.wait_ge(put[b], 64 * STEPS)
                        pool.nop(nofuse=True)

                @block.vector
                def _(dve):
                    chain = Chain(dve, s_dve)

                    def step(i, first, last):
                        chain.step(i)
                        for b in range(2):
                            g = 2 * i + b
                            wide = [P, G, D]
                            v = ag[:, b, :, :]
                            dve.wait_ge(a_in[b], 16 * i + 16)
                            chain.mark(nc.vector.tensor_tensor(v, v, a_row[:].unsqueeze(1).broadcast_to(wide), ALU.mult))
                            chain.after()
                            chain.mark(nc.vector.tensor_tensor(v, v, b_row[:].unsqueeze(1).broadcast_to(wide), ALU.add))
                            chain.after()
                            dve.wait_ge(x_in[b], 64 * i + 64)
                            chain.mark(nc.vector.scalar_tensor_tensor(v, v, 0.0, xs[:, b, :, :], ALU.max, ALU.add))
                            chain.after()
                            for j in range(G):
                                ins = nc.vector.bn_stats(bstats[:, j, :], ag[:, b, j, :])
                            chain.mark(ins)
                            chain.after()
                            if not first:
                                dve.wait_ge(y_ready, g - 1)
                            dve.nop(nofuse=True)
                            for j in range(G):
                                ins = nc.vector.bn_aggr(aggr[:, b, j, :], bstats[:, j, :])
                            chain.mark(ins)
                            chain.after()
                            nc.vector.tensor_scalar(sd[:, b, :], aggr[:, b, :, 1], EPS, None, ALU.add).then_inc(aggr_ready, 1)
                            dve.wait_ge(sd_ready, g + 1)
                            chain.mark(nc.vector.reciprocal(rstd[:, b, :], sd[:, b, :]))
                            chain.after()
                            nc.vector.scalar_tensor_tensor(shift[:, b, :], aggr[:, b, :, 0], -1.0, rstd[:, b, :], ALU.mult, ALU.mult).then_inc(norm_ready, 1)
                    loop(dve, STEPS, step)

                @block.scalar
                def _(act):
                    def step(i, first, last):
                        for b in range(2):
                            g = 2 * i + b
                            act.wait_ge(aggr_ready, g + 1)
                            nc.scalar.activation(sd[:, b, :], sd[:, b, :], ACT.Sqrt).then_inc(sd_ready, 1)
                            act.wait_ge(norm_ready, g + 1)
                            if not first:
                                act.wait_ge(put[b], 64 * i)
                            for j in range(G):
                                ins = nc.scalar.activation(yo[:, b, j, :], ag[:, b, j, :], ACT.Identity,
                                                           bias=shift[:, b, j:j + 1], scale=rstd[:, b, j:j + 1])
                            ins.then_inc(y_ready, 1)
                    loop(act, STEPS, step)


_INS = ['x', 'src', 'dst', 'L0_gnn_thetas', 'L0_gnn_phis', 'L0_gnn_gammas', 'L0_gnn_betas']


def kernel(**inputs):
    import numpy as _np
    import concourse.bacc as _bacc
    from concourse import mybir as _mybir
    from concourse.bass_utils import run_bass_kernel_spmd as _run

    nc = _bacc.Bacc("TRN2", target_bir_lowering=False, num_devices=1)
    arrays, args = {}, []
    for name in _INS:
        a = _np.ascontiguousarray(inputs[name])
        arrays[f"in_{name}_dram"] = a
        args.append(nc.dram_tensor(f"in_{name}_dram", a.shape, _mybir.dt.from_np(a.dtype), kind="ExternalInput").ap())
    args.append(nc.dram_tensor("out_0_dram", inputs['x'].shape, _mybir.dt.float32, kind="ExternalOutput").ap())
    gnn_program(nc, *args)
    r = _run(nc, [arrays], core_ids=[0])
    return r.results[0]["out_0_dram"]
```

```python
import concourse.bass as bass
from concourse import mybir
from contextlib import ExitStack


def loop(engine, count, step, peeled=1):
    head = min(peeled, count - 1)
    for i in range(head):
        step(i, i == 0, False)
    if count - 1 > head:
        with engine.Fori(head, count - 1) as i:
            step(i, False, False)
    step(count - 1, count == 1, True)


class Chain:

    def __init__(self, engine, sem):
        self.engine, self.sem, self.base, self.count, self.per_step = engine, sem, 0, 0, None

    def step(self, i):
        if self.per_step is None and self.count:
            self.per_step = self.count
        self.base = 0 if self.per_step is None else i * self.per_step
        self.count = 0

    def mark(self, instruction):
        self.count += 1
        instruction.then_inc(self.sem, 1)

    def after(self):
        self.engine.wait_ge(self.sem, self.base + self.count)


def gnn_program(nc, x, src, dst, thetas, phis, gammas, betas, out):
    f32, i32 = mybir.dt.float32, mybir.dt.int32
    f16, bf16, f32r = mybir.dt.float16, mybir.dt.bfloat16, mybir.dt.float32r
    ALU = mybir.AluOpType
    ACT = mybir.ActivationFunctionType
    AX_X = mybir.AxisListType.X

    P = 128
    N, D = x.shape
    E = src.shape[0]
    LAYERS = thetas.shape[0]
    KD = D // P
    EPS = 1e-5
    EP = -(-E // 1024) * 1024
    NT = EP // P
    TC = NT // 2
    G = 4
    GE = G * P
    STEPS = EP // (2 * GE)
    NG = 2 * STEPS
    LOW = 512
    LOW_BITS = 9
    HC = -(-(N + 1) // (2 * LOW))
    HIGHS = 2 * HC
    PAD_KEY = N
    ABSENT = EP
    START_PENALTY = -2e38
    END_PENALTY = -1e30
    SKIP = float(1 << 20)
    assert HC <= P and TC <= P and D == KD * P and N < (1 << 20)

    R = 6
    BLOCK_ROWS = P * R
    BLOCKS = N // BLOCK_ROWS
    BLOCK_STEPS = BLOCKS // 4
    REST = N - BLOCKS * BLOCK_ROWS
    RR = max((r for r in range(2, R + 1, 2) if REST % r == 0 and REST // r <= P), default=0)
    assert (REST == 0 or RR) and STEPS > 2 and BLOCK_STEPS > STEPS

    src_row = nc.dram_tensor("src_row", (EP,), f32).ap()
    high_row = nc.dram_tensor("high_row", (EP,), f32).ap()
    position_table = nc.dram_tensor("position_table", (HIGHS * LOW, 1), i32).ap()
    sorted_meta = nc.dram_tensor("sorted_meta", (EP, 4), i32).ap()
    sorted_row = nc.dram_tensor("sorted_row", (EP + 2,), f32).ap()
    start_row = nc.dram_tensor("start_row", (EP,), bf16).ap()
    end_row = nc.dram_tensor("end_row", (EP,), bf16).ap()
    agg_rows = [nc.dram_tensor(f"agg_rows{l}", (EP + 1, D), f32).ap() for l in range(LAYERS - 1)]
    agg_cols = [nc.dram_tensor(f"agg_cols{l}", (NG, P, KD * GE), f32).ap() for l in range(LAYERS)]
    done_rows = nc.dram_tensor("done_rows", (EP, D), f32).ap()

    whole = ExitStack()
    with whole:
        def sb(name, shape, dt, ctx=whole):
            return ctx.enter_context(nc.sbuf_tensor(name, shape, dt))

        def pb(name, shape, dt, ctx=whole):
            return ctx.enter_context(nc.psum_tensor(name, shape, dt))

        sort_signals, sorting_done = [], ExitStack()

        def signal(name):
            sort_signals.append(sorting_done.enter_context(nc.semaphore(name)))
            return sort_signals[-1]

        ident = sb("ident", [P, P], f32)
        ones = sb("ones", [P, P], f32)
        ones_bf = sb("ones_bf", [3, P], bf16)
        gat_src = sb("gat_src", [P, NT], i32)
        gat_dst = sb("gat_dst", [P, NT], i32)
        gat_pos = sb("gat_pos", [P, NT], i32)
        put_src = sb("put_src", [P, NT], i32)
        bn_a = sb("bn_a", [P, KD], f32)
        bn_b = sb("bn_b", [P, KD], f32)
        gam = sb("gam", [P, KD, LAYERS], f32)
        bet = sb("bet", [P, KD, LAYERS], f32)

        sorting = ExitStack()
        with sorting:
            src_col = sb("src_col", [P, NT], f32, sorting)
            low_col = sb("low_col", [P, NT], f32, sorting)
            high_col = sb("high_col", [P, NT], f32, sorting)
            meta = sb("meta", [P, NT, 2], i32, sorting)
            iota_low = sb("iota_low", [P, LOW], f16, sorting)
            iota_high = sb("iota_high", [P, HIGHS], f16, sorting)
            iota_part = sb("iota_part", [P, 2], f32, sorting)
            earlier = sb("earlier", [P, GE], f16, sorting)
            below = sb("below", [P, P], f32, sorting)
            first_pos = sb("first_pos", [HC, 2, LOW], f32, sorting)
            counts = [pb(f"counts{c}", [HC, LOW], f32, sorting) for c in range(2)]

            with ExitStack() as ctx:
                raw = sb("raw", [TC, 2, 2, P], i32, ctx)
                rawf = sb("rawf", [TC, 2, 2, P], f32, ctx)
                high_i = sb("high_i", [TC, 2, P], i32, ctx)
                high_f = sb("high_f", [TC, 2, P], f32, ctx)
                col_i = sb("col_i", [P, 3, NT], i32, ctx)
                zrow = sb("zrow", [1, D], f32, ctx)
                tp = [pb(f"tp{s}", [P, NT], f32, ctx) for s in range(2)]
                s_fill = signal("s_fill")
                s_raw = whole.enter_context(nc.semaphore("s_raw"))
                s_const = signal("s_const")
                s_pool = signal("s_pool")
                s_rawf = signal("s_rawf")
                s_tp = signal("s_tp")
                s_dve = signal("s_dve")
                s_out = whole.enter_context(nc.semaphore("s_out"))
                s_high = signal("s_high")
                loads = [0]
                with nc.Block() as block:
                    @block.sync
                    def _(sp):
                        sp.wait_ge(s_fill, 1)
                        for which, edges in enumerate((src, dst)):
                            for c in range(2):
                                full = max(min(E // P - c * TC, TC), 0)
                                if full:
                                    sp.dma_start(raw[0:full, which, c, :], edges[c * TC * P:(c * TC + full) * P]
                                                 .rearrange("(t p) -> t p", p=P)).then_inc(s_raw, 16)
                                    loads[0] += 16
                                if full < TC and E % P and full == E // P - c * TC:
                                    sp.dma_start(raw[full:full + 1, which, c, 0:E % P],
                                                 edges[E - E % P:E].unsqueeze(0)).then_inc(s_raw, 16)
                                    loads[0] += 16
                        with nc.allow_non_contiguous_dma(reason="small, once"):
                            for k in range(KD):
                                for l in range(LAYERS):
                                    sp.dma_start(gam[:, k, l:l + 1], gammas[l, k * P:(k + 1) * P].unsqueeze(1)).then_inc(s_out, 16)
                                    sp.dma_start(bet[:, k, l:l + 1], betas[l, k * P:(k + 1) * P].unsqueeze(1)).then_inc(s_out, 16)
                        sp.wait_ge(s_rawf, 1)
                        sp.dma_start(src_row.rearrange("(c t p) -> t c p", c=2, p=P), rawf[:, 0, :, :]).then_inc(s_out, 16)
                        sp.wait_ge(s_high, 1)
                        sp.dma_start(high_row.rearrange("(c t p) -> t c p", c=2, p=P), high_f[:, :, :]).then_inc(s_out, 16)
                        sp.wait_ge(s_const, 1)
                        for l in range(LAYERS - 1):
                            sp.dma_start(agg_rows[l][ABSENT:ABSENT + 1, :], zrow[:, :]).then_inc(s_out, 16)
                        sp.wait_ge(s_out, 16 * (2 * KD * LAYERS + 2 + LAYERS - 1))

                    @block.gpsimd
                    def _(pool):
                        chain = Chain(pool, s_pool)
                        nc.gpsimd.memset(raw[:, 1, :, :], 0)
                        nc.gpsimd.memset(raw[:, 0, :, :], PAD_KEY).then_inc(s_fill, 1)
                        nc.gpsimd.memset(zrow[:], 0.0)
                        nc.gpsimd.memset(ones_bf[:], 1.0)
                        nc.gpsimd.memset(ones[:], 1.0)
                        nc.gpsimd.memset(ident[:], 0.0)
                        nc.gpsimd.memset(below[:], 1.0)
                        chain.mark(nc.gpsimd.memset(earlier[:], 1.0))
                        chain.after()
                        nc.gpsimd.affine_select(out=ident[:], in_=ident[:], compare_op=ALU.not_equal, fill=1.0, base=0,
                                                pattern=[[1, P]], channel_multiplier=-1)
                        nc.gpsimd.affine_select(out=below[:], in_=below[:], compare_op=ALU.is_gt, fill=0.0, base=0,
                                                pattern=[[1, P]], channel_multiplier=-1)
                        nc.gpsimd.affine_select(out=earlier[:, GE - P:GE], in_=earlier[:, GE - P:GE], compare_op=ALU.is_gt,
                                                fill=0.0, base=0, pattern=[[-1, P]], channel_multiplier=1)
                        nc.gpsimd.iota(iota_low[:], [[1, LOW]], base=0, channel_multiplier=0, allow_small_or_imprecise_dtypes=True)
                        nc.gpsimd.iota(iota_high[:], [[1, HIGHS]], base=0, channel_multiplier=0, allow_small_or_imprecise_dtypes=True)
                        nc.gpsimd.iota(iota_part[:], [[HC, 2]], base=0, channel_multiplier=1,
                                       allow_small_or_imprecise_dtypes=True).then_inc(s_const, 1)

                    @block.vector
                    def _(dve):
                        chain = Chain(dve, s_dve)
                        dve.wait_ge(s_raw, loads[0])
                        nc.vector.tensor_copy(rawf[:], raw[:]).then_inc(s_rawf, 1)
                        chain.mark(nc.vector.tensor_single_scalar(high_i[:], raw[:, 0, :, :], LOW_BITS, ALU.logical_shift_right))
                        chain.after()
                        nc.vector.tensor_copy(high_f[:], high_i[:]).then_inc(s_high, 1)
                        dve.wait_ge(s_tp, 1)
                        nc.vector.tensor_copy(src_col[:], tp[0][:, :])
                        nc.vector.tensor_copy(meta[:, :, 0], tp[0][:, :])
                        nc.vector.tensor_copy(meta[:, :, 1], tp[1][:, :])
                        chain.mark(nc.vector.tensor_copy(col_i[:, 0, :], tp[0][:, :]))
                        chain.after()
                        nc.vector.tensor_single_scalar(col_i[:, 1, :], col_i[:, 0, :], LOW_BITS, ALU.logical_shift_right)
                        chain.mark(nc.vector.tensor_single_scalar(col_i[:, 2, :], col_i[:, 0, :], LOW - 1, ALU.bitwise_and))
                        chain.after()
                        nc.vector.tensor_copy(high_col[:], col_i[:, 1, :])
                        nc.vector.tensor_copy(low_col[:], col_i[:, 2, :])

                    @block.tensor
                    def _(pe):
                        pe.wait_ge(s_const, 1)
                        pe.wait_ge(s_rawf, 1)
                        for which in range(2):
                            for c in range(2):
                                last = nc.tensor.transpose(tp[which][:, c * TC:(c + 1) * TC], rawf[:, which, c, :], ident[0:TC, 0:TC])
                        last.then_inc(s_tp, 1)

            with ExitStack() as ctx:
                hot_high = sb("hot_high", [P, 2, G, HIGHS], f16, ctx)
                hot_low = sb("hot_low", [P, 2, G, LOW], f16, ctx)
                incl = sb("incl", [HC, 2, LOW], f32, ctx)
                cnt = sb("cnt", [HC, 2, LOW], f32, ctx)
                ones_low = sb("ones_low", [HC, LOW], f32, ctx)
                base = sb("base", [HC, 2], f32, ctx)
                table = sb("table", [HC, 2, LOW], i32, ctx)
                base_ps = pb("base_ps", [HC, 2], f32, ctx)
                hot_ready = signal("hot_ready")
                hot_used = signal("hot_used")
                s_tot = signal("s_tot")
                s_base = signal("s_base")
                s_dve = signal("s_dve2")
                s_table = signal("s_table")
                s_stored = whole.enter_context(nc.semaphore("s_stored"))
                with nc.Block() as block:
                    @block.vector
                    def _(dve):
                        def step(i, first, last):
                            for b in range(2):
                                g = 2 * i + b
                                if not first:
                                    dve.wait_ge(hot_used, g - 1)
                                for j in range(G):
                                    t = G * g + j
                                    nc.vector.tensor_scalar(hot_high[:, b, j, :], iota_high[:], high_col[:, bass.ds(t, 1)], None, ALU.is_equal)
                                    ins = nc.vector.tensor_scalar(hot_low[:, b, j, :], iota_low[:], low_col[:, bass.ds(t, 1)], None, ALU.is_equal)
                                ins.then_inc(hot_ready, 1)
                        loop(dve, STEPS, step)

                        chain = Chain(dve, s_dve)
                        nc.vector.memset(ones_low[:], 1.0)
                        dve.wait_ge(hot_used, NG)
                        for c in range(2):
                            chain.mark(nc.vector.tensor_copy(cnt[:, c, :], counts[c][:, :]))
                        chain.after()
                        for c in range(2):
                            ins = nc.vector.tensor_tensor_scan(incl[:, c, :], ones_low[:], cnt[:, c, :], 0.0, ALU.mult, ALU.add)
                        ins.then_inc(s_tot, 1)
                        dve.wait_ge(s_base, 1)
                        chain.mark(nc.vector.tensor_copy(base[:], base_ps[:]))
                        chain.after()
                        for c in range(2):
                            chain.mark(nc.vector.tensor_scalar(incl[:, c, :], incl[:, c, :], base[:, c:c + 1], None, ALU.add))
                        chain.after()
                        chain.mark(nc.vector.tensor_tensor(first_pos[:], incl[:], cnt[:], ALU.subtract))
                        chain.after()
                        chain.mark(nc.vector.tensor_scalar(incl[:], incl[:], -1.0 - ABSENT, None, ALU.add))
                        chain.after()
                        chain.mark(nc.vector.scalar_tensor_tensor(cnt[:], cnt[:], 0.0, incl[:], ALU.is_gt, ALU.mult))
                        chain.after()
                        nc.vector.tensor_scalar(table[:], cnt[:], float(ABSENT), None, ALU.add).then_inc(s_table, 1)

                    @block.tensor
                    def _(pe):
                        def step(i, first, last):
                            for b in range(2):
                                g = 2 * i + b
                                pe.wait_ge(hot_ready, g + 1)
                                for j in range(G):
                                    for c in range(2):
                                        ins = nc.tensor.matmul(counts[c][:, :], hot_high[:, b, j, c * HC:(c + 1) * HC], hot_low[:, b, j, :],
                                                               start=(first and b == 0 and j == 0), stop=(last and b == 1 and j == G - 1),
                                                               skip_group_check=True)
                                ins.then_inc(hot_used, 1)
                        loop(pe, STEPS, step)
                        pe.wait_ge(s_tot, 1)
                        nc.tensor.matmul(base_ps[:, 0:1], below[0:HC, 0:HC], incl[:, 0, LOW - 1:LOW], start=True, stop=True)
                        nc.tensor.matmul(base_ps[:, 1:2], below[0:HC, 0:HC], incl[:, 1, LOW - 1:LOW], start=True, stop=False)
                        nc.tensor.matmul(base_ps[:, 1:2], ones[0:HC, 0:HC], incl[:, 0, LOW - 1:LOW], start=False, stop=True).then_inc(s_base, 1)

                    @block.sync
                    def _(sp):
                        sp.wait_ge(s_table, 1)
                        sp.dma_start(position_table.rearrange("(c h l) o -> h c (l o)", c=2, l=LOW), table[:]).then_inc(s_stored, 16)
                        sp.wait_ge(s_stored, 16)

            with ExitStack() as ctx:
                hot_high = sb("hot_high2", [P, 2, G, HIGHS], f16, ctx)
                hot_low = sb("hot_low2", [P, 2, G, LOW], f16, ctx)
                hot_rows = sb("hot_rows", [HC, 2, 2, GE], f16, ctx)
                keys = sb("keys", [P, 2, GE], f32, ctx)
                highs = sb("highs", [HC, 2, GE], f32, ctx)
                c_hi = sb("c_hi", [HC, 2, 2, LOW], f16, ctx)
                c_lo = sb("c_lo", [HC, 2, 2, LOW], f16, ctx)
                junk = sb("junk", [P, G, LOW], f16, ctx)
                junk2 = sb("junk2", [P, G, LOW], f16, ctx)
                same = sb("same", [P, 2, G], f32, ctx)
                before = sb("before", [P, 2, G], f32, ctx)
                pos = sb("pos", [P, 2, G], i32, ctx)
                row = sb("row", [P, 2, G, 4], i32, ctx)
                idx = sb("idx", [P, 2, G], i32, ctx)
                found = [pb(f"found{j}", [P, LOW], f32, ctx) for j in range(G)]
                names = ("hi_ready", "lo_ready", "rows_ready", "hot_ready2", "found_ready", "found_used", "next_ready",
                         "row_ready", "pos_ready", "keys_used", "s_dve3")
                (hi_ready, lo_ready, rows_ready, hot_ready, found_ready, found_used, next_ready,
                 row_ready, pos_ready, keys_used, s_dve) = [signal(n) for n in names]
                keys_in = [whole.enter_context(nc.semaphore(f"keys_in{b}")) for b in range(2)]
                looked_up = [whole.enter_context(nc.semaphore(f"looked_up{b}")) for b in range(2)]
                scattered = [whole.enter_context(nc.semaphore(f"scattered{b}")) for b in range(2)]
                with nc.Block() as block:
                    @block.sync
                    def _(sp):
                        def step(i, first, last):
                            for b in range(2):
                                g = 2 * i + b
                                if not first:
                                    sp.wait_ge(keys_used, g - 1)
                                sp.dma_start(keys[:, b, :], src_row[bass.ds(g * GE, GE)].partition_broadcast(P)).then_inc(keys_in[b], 16)
                                sp.dma_start(highs[:, b, :], high_row[bass.ds(g * GE, GE)].partition_broadcast(HC)).then_inc(keys_in[b], 16)
                        loop(sp, STEPS, step)

                    @block.scalar
                    def _(act):
                        def step(i, first, last):
                            for b in range(2):
                                g = 2 * i + b
                                act.wait_ge(next_ready, g + 1)
                                if not first:
                                    act.wait_ge(found_ready, G * (g - 1))
                                for c in range(2):
                                    ins = nc.scalar.copy(c_hi[:, b, c, :], counts[c][:, :])
                                ins.then_inc(hi_ready, 1)
                        loop(act, STEPS, step)

                    @block.tensor
                    def _(pe):
                        for c in range(2):
                            ins = nc.tensor.matmul(counts[c][:, :], ident[0:HC, 0:HC], first_pos[:, c, :], start=True, stop=False,
                                                   skip_group_check=True)
                        ins.then_inc(next_ready, 1)

                        def step(i, first, last):
                            for b in range(2):
                                g = 2 * i + b
                                pe.wait_ge(rows_ready, g + 1)
                                pe.wait_ge(hi_ready, g + 1)
                                pe.wait_ge(lo_ready, g + 1)
                                for j in range(G):
                                    if not (first and b == 0):
                                        pe.wait_ge(found_used, G * (g - 1) + j + 1)
                                    n = 0
                                    for c in range(2):
                                        for part in (c_hi, c_lo):
                                            ins = nc.tensor.matmul(found[j][:, :], hot_rows[:, b, c, j * P:(j + 1) * P], part[:, b, c, :],
                                                                   start=(n == 0), stop=(n == 3))
                                            n += 1
                                    ins.then_inc(found_ready, 1)
                                pe.wait_ge(hot_ready, g + 1)
                                for j in range(G):
                                    for c in range(2):
                                        ins = nc.tensor.matmul(counts[c][:, :], hot_high[:, b, j, c * HC:(c + 1) * HC], hot_low[:, b, j, :],
                                                               start=False, stop=(last and b == 1 and j == G - 1), skip_group_check=True)
                                ins.then_inc(next_ready, 1)
                        loop(pe, STEPS, step)

                    @block.vector
                    def _(dve):
                        chain = Chain(dve, s_dve)

                        def step(i, first, last):
                            chain.step(i)
                            for b in range(2):
                                g = 2 * i + b
                                dve.wait_ge(keys_in[b], 32 * i + 32)
                                if not first:
                                    dve.wait_ge(found_ready, G * (g - 1))
                                    dve.wait_ge(next_ready, g)
                                for c in range(2):
                                    ins = nc.vector.tensor_scalar(hot_rows[:, b, c, :], highs[:, b, :], iota_part[0:HC, c:c + 1], None, ALU.is_equal)
                                ins.then_inc(rows_ready, 1)
                                dve.wait_ge(hi_ready, g + 1)
                                for c in range(2):
                                    ins = nc.vector.tensor_tensor(c_lo[:, b, c, :], counts[c][:, :], c_hi[:, b, c, :], ALU.subtract)
                                ins.then_inc(lo_ready, 1)
                                for j in range(G):
                                    t = G * g + j
                                    nc.vector.tensor_scalar(hot_high[:, b, j, :], iota_high[:], high_col[:, bass.ds(t, 1)], None, ALU.is_equal)
                                    ins = nc.vector.tensor_scalar(hot_low[:, b, j, :], iota_low[:], low_col[:, bass.ds(t, 1)], None, ALU.is_equal)
                                ins.then_inc(hot_ready, 1)
                                if not first:
                                    dve.wait_ge(scattered[b], 64 * i)
                                nc.vector.tensor_copy(row[:, b, :, 0:2], meta[:, bass.ds(G * g, G), :])
                                nc.vector.memset(row[:, b, :, 3], 0)
                                nc.vector.tensor_copy(idx[:, b, :], meta[:, bass.ds(G * g, G), 1]).then_inc(row_ready, 1)
                                for j in range(G):
                                    t = G * g + j
                                    wide = (j + 1) * P
                                    ins = nc.vector.scalar_tensor_tensor(junk[:, j, 0:wide], keys[:, b, 0:wide], src_col[:, bass.ds(t, 1)],
                                                                         earlier[:, GE - wide:GE], ALU.is_equal, ALU.mult,
                                                                         accum_out=same[:, b, j:j + 1])
                                ins.then_inc(keys_used, 1)
                                dve.wait_ge(keys_used, g + 1)
                                for j in range(G):
                                    dve.wait_ge(found_ready, G * g + j + 1)
                                    ins = nc.vector.scalar_tensor_tensor(junk2[:, j, :], found[j][:, :], 1.0, hot_low[:, b, j, :], ALU.mult, ALU.mult,
                                                                         accum_out=before[:, b, j:j + 1])
                                    ins.then_inc(found_used, 1)
                                dve.wait_ge(found_used, G * g + G)
                                nc.vector.tensor_tensor(pos[:, b, :], same[:, b, :], before[:, b, :], ALU.add).then_inc(pos_ready, 1)
                        loop(dve, STEPS, step)

                    @block.gpsimd
                    def _(pool):
                        def step(i, first, last):
                            for b in range(2):
                                g = 2 * i + b
                                pool.wait_ge(row_ready, g + 1)
                                pool.nop(nofuse=True)
                                for j in range(G):
                                    nc.gpsimd.indirect_dma_start(row[:, b, j, 2:3], None, position_table[:, :],
                                                                 bass.IndirectOffsetOnAxis(ap=idx[:, b, j:j + 1], axis=0)).then_inc(looked_up[b], 16)
                                pool.wait_ge(looked_up[b], 64 * i + 64)
                                pool.wait_ge(pos_ready, g + 1)
                                pool.nop(nofuse=True)
                                for j in range(G):
                                    nc.gpsimd.indirect_dma_start(sorted_meta[:, :], bass.IndirectOffsetOnAxis(ap=pos[:, b, j:j + 1], axis=0),
                                                                 row[:, b, j, :], None).then_inc(scattered[b], 16)
                        loop(pool, STEPS, step)
                        for b in range(2):
                            pool.wait_ge(scattered[b], 64 * STEPS)
                            pool.nop(nofuse=True)

        layering = ExitStack()
        mask = sb("mask", [P, EP], bf16, layering)

        with ExitStack() as ctx:
            sm = sb("sm", [TC, 2, P, 4], i32, ctx)
            here = sb("here", [TC, 2, P], f32, ctx)
            prev = sb("prev", [TC, 2, P], f32, ctx)
            nxt = sb("nxt", [TC, 2, P], f32, ctx)
            cols = sb("cols", [TC, 4, 2, P], f32, ctx)
            flag = sb("flag", [TC, 2, P], f32, ctx)
            pen = sb("pen", [TC, 2, 2, P], bf16, ctx)
            edge = sb("edge", [1, 2], f32, ctx)
            tp = [pb(f"tq{s}", [P, NT], f32, ctx) for s in range(4)]
            (here_ready, edge_ready, pens_ready, cols_ready, tp_ready, s_dve) = [
                signal(n) for n in ("here_ready", "edge_ready", "pens_ready", "cols_ready", "tp_ready", "s_dve4")]
            m_in, row_out, shift_in, pens_out, mask_in = [whole.enter_context(nc.semaphore(n))
                                                          for n in ("m_in", "row_out", "shift_in", "pens_out", "mask_in")]
            with nc.Block() as block:
                @block.sync
                def _(sp):
                    sp.dma_start(sm[:].rearrange("t c p m -> t c (p m)"), sorted_meta.rearrange("(c t p) m -> t c (p m)", c=2, p=P)).then_inc(m_in, 16)
                    sp.wait_ge(edge_ready, 1)
                    sp.dma_start(sorted_row[0:1].unsqueeze(0), edge[:, 0:1]).then_inc(row_out, 16)
                    sp.dma_start(sorted_row[EP + 1:EP + 2].unsqueeze(0), edge[:, 1:2]).then_inc(row_out, 16)
                    sp.wait_ge(here_ready, 1)
                    sp.dma_start(sorted_row[1:EP + 1].rearrange("(c t p) -> t c p", c=2, p=P), here[:]).then_inc(row_out, 16)
                    sp.wait_ge(row_out, 48)
                    sp.dma_start(prev[:], sorted_row[0:EP].rearrange("(c t p) -> t c p", c=2, p=P)).then_inc(shift_in, 16)
                    sp.dma_start(nxt[:], sorted_row[2:EP + 2].rearrange("(c t p) -> t c p", c=2, p=P)).then_inc(shift_in, 16)
                    sp.wait_ge(pens_ready, 1)
                    sp.dma_start(start_row.rearrange("(c t p) -> t c p", c=2, p=P), pen[:, 0, :, :]).then_inc(pens_out, 16)
                    sp.dma_start(end_row.rearrange("(c t p) -> t c p", c=2, p=P), pen[:, 1, :, :]).then_inc(pens_out, 16)
                    sp.wait_ge(pens_out, 32)
                    sp.dma_start(mask[:], start_row.partition_broadcast(P)).then_inc(mask_in, 16)
                    sp.wait_ge(mask_in, 16)

                @block.vector
                def _(dve):
                    chain = Chain(dve, s_dve)
                    nc.vector.memset(edge[:, 0:1], -1.0)
                    nc.vector.memset(edge[:, 1:2], float(N + 1)).then_inc(edge_ready, 1)
                    dve.wait_ge(m_in, 16)
                    nc.vector.tensor_copy(here[:], sm[:, :, :, 0]).then_inc(here_ready, 1)
                    nc.vector.tensor_copy(cols[:, 1, :, :], sm[:, :, :, 1])
                    nc.vector.tensor_copy(cols[:, 2, :, :], sm[:, :, :, 2])
                    dve.wait_ge(here_ready, 1)
                    nc.vector.tensor_scalar(cols[:, 0, :, :], here[:], float(N - 1), None, ALU.min)
                    dve.wait_ge(shift_in, 32)
                    chain.mark(nc.vector.tensor_tensor(prev[:], here[:], prev[:], ALU.not_equal))
                    chain.mark(nc.vector.tensor_tensor(nxt[:], here[:], nxt[:], ALU.is_equal))
                    chain.after()
                    nc.vector.tensor_scalar(pen[:, 0, :, :], prev[:], START_PENALTY, None, ALU.mult)
                    chain.mark(nc.vector.scalar_tensor_tensor(flag[:], here[:], float(N), nxt[:], ALU.is_ge, ALU.max))
                    chain.after()
                    nc.vector.tensor_scalar(pen[:, 1, :, :], flag[:], END_PENALTY, None, ALU.mult).then_inc(pens_ready, 1)
                    nc.vector.scalar_tensor_tensor(cols[:, 3, :, :], flag[:], SKIP, here[:], ALU.mult, ALU.add).then_inc(cols_ready, 1)
                    dve.wait_ge(tp_ready, 1)
                    for s, to in enumerate((gat_src, gat_dst, gat_pos, put_src)):
                        nc.vector.tensor_copy(to[:], tp[s][:, :])

                @block.tensor
                def _(pe):
                    pe.wait_ge(cols_ready, 1)
                    for s in range(4):
                        for c in range(2):
                            ins = nc.tensor.transpose(tp[s][:, c * TC:(c + 1) * TC], cols[:, s, c, :], ident[0:TC, 0:TC])
                    ins.then_inc(tp_ready, 1)

        with nc.Block() as block:
            @block.gpsimd
            def _(pool):
                for spent in sort_signals:
                    pool.sem_clear(spent)
        sorting_done.close()

        w_in, w_t, w_ev, sd_ready, var_ready = [whole.enter_context(nc.semaphore(n)) for n in
                                                ("w_in", "w_t", "w_ev", "sd_ready", "var_ready")]
        for layer in range(LAYERS):
            one = layer == 0
            more = layer < LAYERS - 1
            with ExitStack() as ctx:
                L = str(layer)
                w_raw = sb("w_raw" + L, [P, 2, KD, D], f32, ctx)
                w_full = sb("w_full" + L, [P, 2, KD, D], f32, ctx)
                w_high = sb("w_high" + L, [P, 2, KD, D], f32r, ctx)
                w_low = sb("w_low" + L, [P, 2, KD, D], f32r, ctx)
                fresh = sb("fresh" + L, [P, 2, G, D], f32, ctx)
                own = sb("own" + L, [P, 2, G, D], f32, ctx)
                idx = sb("idx" + L, [P, 2, 2, G], i32, ctx)
                pen = sb("pen" + L, [1, 2, GE], bf16, ctx)
                x_full = None if one else sb("x_full" + L, [P, 2, 2, KD, GE], f32, ctx)
                x_high = sb("x_high" + L, [P, 2, 2, KD, GE], f32r, ctx)
                x_low = sb("x_low" + L, [P, 2, 2, KD, GE], f32r, ctx)
                top = sb("top" + L, [P, 2, KD, GE], f32, ctx)
                summ = sb("summ" + L, [P, 2, KD, GE], f32, ctx)
                agg = sb("agg" + L, [P, 2, KD, GE], f32, ctx)
                sq = sb("sq" + L, [P, GE], f32, ctx)
                rows = sb("rows" + L, [P, 2, G, D], f32, ctx)
                sums = sb("sums" + L, [P, 2, KD, NG], f32, ctx)
                stat = sb("stat" + L, [P, 6, KD], f32, ctx)
                xt_ps = pb("xt_ps" + L, [P, KD, GE], f32, ctx)
                y_ps = [pb(f"y_ps{m}" + L, [P, GE], f32, ctx) for m in range(KD)]
                z_ps = [pb(f"z_ps{m}" + L, [P, GE], f32, ctx) for m in range(KD)]
                row_ps = pb("row_ps" + L, [P, G, D], f32, ctx)
                names = ["idx_ready", "j_turned", "j_high", "j_ready", "i_high", "i_ready", "yz_ready", "sum_ready",
                         "agg_ready", "sq_ready", "row_turned", "row_ready", "s_dve"] + (["i_turned"] if one else ["j_full", "i_full"])
                signals = [whole.enter_context(nc.semaphore(n + L)) for n in names]
                (idx_ready, j_turned, j_high, j_ready, i_high, i_ready, yz_ready, sum_ready,
                 agg_ready, sq_ready, row_turned, row_ready, s_dve) = signals[:13]
                i_turned, (j_full, i_full) = (signals[13], (None, None)) if one else (None, signals[13:])
                j_in, i_in, pen_in, agg_out, row_out = [[whole.enter_context(nc.semaphore(f"{n}{b}_{L}")) for b in range(2)]
                                                        for n in ("j_in", "i_in", "pen_in", "agg_out", "row_out")]
                with nc.Block() as block:
                    @block.gpsimd
                    def _(pool):
                        def step(i, first, last):
                            for b in range(2):
                                g = 2 * i + b
                                if not first:
                                    pool.wait_ge(j_turned, g - 1)
                                    if one:
                                        pool.wait_ge(i_turned, g - 1)
                                    pool.nop(nofuse=True)
                                cols = gat_dst if one else gat_pos
                                ins = nc.gpsimd.tensor_copy(idx[:, b, 0, :], cols[:, bass.ds(G * g, G)])
                                if one:
                                    ins = nc.gpsimd.tensor_copy(idx[:, b, 1, :], gat_src[:, bass.ds(G * g, G)])
                                ins.then_inc(idx_ready, 1)
                                pool.wait_ge(idx_ready, g + 1)
                                pool.nop(nofuse=True)
                                from_ = x if one else agg_rows[layer - 1]
                                for j in range(G):
                                    nc.gpsimd.indirect_dma_start(fresh[:, b, j, :], None, from_[:, :],
                                                                 bass.IndirectOffsetOnAxis(ap=idx[:, b, 0, j:j + 1], axis=0)).then_inc(j_in[b], 16)
                                if one:
                                    for j in range(G):
                                        nc.gpsimd.indirect_dma_start(own[:, b, j, :], None, x[:, :],
                                                                     bass.IndirectOffsetOnAxis(ap=idx[:, b, 1, j:j + 1], axis=0)).then_inc(i_in[b], 16)
                        loop(pool, STEPS, step)

                    @block.sync
                    def _(sp):
                        sp.dma_start(w_raw[:, 0, :, :], thetas[layer].rearrange("(m o) i -> o m i", o=P)).then_inc(w_in, 16)
                        sp.dma_start(w_raw[:, 1, :, :], phis[layer].rearrange("(m o) i -> o m i", o=P)).then_inc(w_in, 16)

                        def load_pen(g, b):
                            sp.dma_start(pen[:, b, :], end_row[bass.ds(g * GE, GE)].unsqueeze(0)).then_inc(pen_in[b], 16)

                        def load_own(g, b):
                            if not one:
                                sp.dma_start(own[:, b, :, :].rearrange("p a d -> p (a d)"),
                                             agg_cols[layer - 1][bass.ds(g, 1), :, :].rearrange("a p f -> p (a f)")).then_inc(i_in[b], 16)

                        for b in range(2):
                            load_own(b, b)
                            load_pen(b, b)

                        def store_rows(g, b):
                            sp.wait_ge(row_ready, g + 1)
                            sp.dma_start(agg_rows[layer][bass.ds(g * GE, GE), :].rearrange("(a p) d -> p a d", p=P), rows[:, b, :, :]).then_inc(row_out[b], 16)

                        def step(i, first, last):
                            for b in range(2):
                                g = 2 * i + b
                                if not last:
                                    if not one:
                                        sp.wait_ge(i_full, g + 1)
                                        load_own(g + 2, b)
                                    sp.wait_ge(yz_ready, 2 * g + 2)
                                    load_pen(g + 2, b)
                                sp.wait_ge(agg_ready, 2 * g + 2)
                                sp.dma_start(agg_cols[layer][bass.ds(g, 1), :, :].rearrange("a p f -> p (a f)"),
                                             agg[:, b, :, :].rearrange("p k f -> p (k f)")).then_inc(agg_out[b], 16)
                                if more and not (first and b == 0):
                                    store_rows(g - 1, 1 - b)
                        loop(sp, STEPS, step)
                        if more:
                            store_rows(NG - 1, 1)
                        for b in range(2):
                            if more:
                                sp.wait_ge(row_out[b], 16 * STEPS)
                            sp.wait_ge(agg_out[b], 16 * STEPS)

                    @block.tensor
                    def _(pe):
                        pe.wait_ge(w_in, 32 * (layer + 1))
                        for s in range(2):
                            if s == 1:
                                pe.wait_ge(w_ev, 4 * layer + 1)
                            for m in range(KD):
                                for k in range(KD):
                                    ins = nc.tensor.transpose(xt_ps[:, k, m * P:(m + 1) * P], w_raw[:, s, m, k * P:(k + 1) * P], ident[:])
                            ins.then_inc(w_t, 1)

                        def turn(rows_, b, signal):
                            for j in range(G):
                                for k in range(KD):
                                    ins = nc.tensor.transpose(xt_ps[:, k, j * P:(j + 1) * P], rows_[:, b, j, k * P:(k + 1) * P], ident[:])
                            ins.then_inc(signal, 1)

                        def turn_j(g, i, b, start):
                            pe.wait_ge(j_in[b], 64 * i + 64)
                            if start:
                                pe.wait_ge(w_ev, 4 * layer + 4)
                            else:
                                pe.wait_ge(i_ready if one else j_full, g)
                            turn(fresh, b, j_turned)

                        def turn_i(g, i, b):
                            pe.wait_ge(i_in[b], 64 * i + 64)
                            pe.wait_ge(j_ready, g + 1)
                            turn(own, b, i_turned)

                        def products(g, i, b, start):
                            pe.wait_ge(j_ready, g + 1)
                            pe.wait_ge(i_ready, g + 1)
                            pe.wait_ge(pen_in[b], 16 * i + 16)
                            for m in range(KD):
                                if not start:
                                    pe.wait_ge(sum_ready, 2 * g - 1 + m)
                                for s, to in enumerate((y_ps[m], z_ps[m])):
                                    for k in range(KD):
                                        out_m = slice(m * P, (m + 1) * P)
                                        nc.tensor.matmul(to[:, :], w_high[:, s, k, out_m], x_high[:, b, s, k, :], start=(k == 0), stop=False)
                                        nc.tensor.matmul(to[:, :], w_high[:, s, k, out_m], x_low[:, b, s, k, :], start=False, stop=False)
                                        nc.tensor.matmul(to[:, :], w_low[:, s, k, out_m], x_high[:, b, s, k, :], start=False,
                                                         stop=(s == 0 and k == KD - 1))
                                nc.tensor.matmul(z_ps[m][:, :], ones_bf[0:1, :], pen[:, b, :], start=False, stop=True).then_inc(yz_ready, 1)

                        def turn_back(g, b, start):
                            pe.wait_ge(agg_ready, 2 * g + 2)
                            if not start:
                                pe.wait_ge(row_ready, g)
                            for j in range(G):
                                for k in range(KD):
                                    ins = nc.tensor.transpose(row_ps[:, j, k * P:(k + 1) * P], agg[:, b, k, j * P:(j + 1) * P], ident[:])
                            ins.then_inc(row_turned, 1)

                        for b in range(2):
                            turn_j(b, 0, b, b == 0)
                            if one:
                                turn_i(b, 0, b)

                        def step(i, first, last):
                            for b in range(2):
                                g = 2 * i + b
                                start = first and b == 0
                                products(g, i, b, start)
                                if not last:
                                    turn_j(g + 2, i + 1, b, False)
                                if more and not start:
                                    turn_back(g - 1, 1 - b, first and b == 1)
                                if not last and one:
                                    turn_i(g + 2, i + 1, b)
                        loop(pe, STEPS, step)
                        if more:
                            turn_back(NG - 1, 1, False)

                    @block.scalar
                    def _(act):
                        def columns(g, i, b, start2):
                            act.wait_ge(j_turned, g + 1)
                            if not start2:
                                act.wait_ge(yz_ready, 2 * g - 2)
                            if one:
                                nc.scalar.copy(x_high[:, b, 0, :, :], xt_ps[:, :, :]).then_inc(j_high, 1)
                                act.wait_ge(i_turned, g + 1)
                                nc.scalar.copy(x_high[:, b, 1, :, :], xt_ps[:, :, :]).then_inc(i_high, 1)
                                return
                            for k in range(KD):
                                ins = nc.scalar.activation(x_full[:, b, 0, k, :], xt_ps[:, k, :], ACT.Relu, bias=bn_b[:, k:k + 1], scale=bn_a[:, k:k + 1])
                            ins.then_inc(j_full, 1)
                            act.wait_ge(i_in[b], 16 * i + 16)
                            own_k = own[:, b, :, :].rearrange("p a d -> p (a d)")
                            for k in range(KD):
                                ins = nc.scalar.activation(x_full[:, b, 1, k, :], own_k[:, k * GE:(k + 1) * GE], ACT.Relu, bias=bn_b[:, k:k + 1], scale=bn_a[:, k:k + 1])
                            ins.then_inc(i_full, 1)
                            act.wait_ge(j_full, g + 1)
                            nc.scalar.copy(x_high[:, b, 0, :, :], x_full[:, b, 0, :, :]).then_inc(j_high, 1)
                            act.wait_ge(i_full, g + 1)
                            nc.scalar.copy(x_high[:, b, 1, :, :], x_full[:, b, 1, :, :]).then_inc(i_high, 1)

                        for b in range(2):
                            columns(b, 0, b, True)

                        def step(i, first, last):
                            for b in range(2):
                                g = 2 * i + b
                                if not last:
                                    columns(g + 2, i + 1, b, False)
                                for m in range(KD):
                                    act.wait_ge(sum_ready, 2 * g + m + 1)
                                    if not first and m == 0:
                                        if more:
                                            act.wait_ge(row_turned, g - 1)
                                        act.wait_ge(agg_out[b], 16 * i)
                                    nc.scalar.activation(agg[:, b, m, :], summ[:, b, m, :], ACT.Relu,
                                                         accum_out=sums[:, 0, m, bass.ds(g, 1)]).then_inc(agg_ready, 1)
                                    act.wait_ge(agg_ready, 2 * g + m + 1)
                                    nc.scalar.activation(sq[:], agg[:, b, m, :], ACT.Square,
                                                         accum_out=sums[:, 1, m, bass.ds(g, 1)]).then_inc(sq_ready, 1)
                        loop(act, STEPS, step)
                        act.wait_ge(var_ready, layer + 1)
                        nc.scalar.activation(stat[:, 3, :], stat[:, 2, :], ACT.Sqrt).then_inc(sd_ready, 1)

                    @block.vector
                    def _(dve):
                        dve.wait_ge(w_t, 2 * layer + 1)
                        nc.vector.tensor_copy(w_full[:, 0, :, :], xt_ps[:, :, 0:D]).then_inc(w_ev, 1)
                        for b in range(2):
                            for m in range(KD):
                                nc.vector.memset(top[:, b, m, GE - 1:GE], 0.0)
                        dve.wait_ge(w_t, 2 * layer + 2)
                        dve.wait_ge(w_ev, 4 * layer + 1)
                        nc.vector.tensor_tensor(w_full[:, 1, :, :], xt_ps[:, :, 0:D], w_full[:, 0, :, :], ALU.subtract).then_inc(w_ev, 1)
                        dve.wait_ge(w_ev, 4 * layer + 2)
                        nc.vector.tensor_copy(w_high[:], w_full[:]).then_inc(w_ev, 1)
                        dve.wait_ge(w_ev, 4 * layer + 3)
                        nc.vector.tensor_tensor(w_low[:], w_full[:], w_high[:].bitcast(f32), ALU.subtract).then_inc(w_ev, 1)

                        def lows(g, b, start2):
                            for s, (high, ready) in enumerate(((j_high, j_ready), (i_high, i_ready))):
                                dve.wait_ge(high, g + 1)
                                if not start2 and s == 0:
                                    dve.wait_ge(yz_ready, 2 * g - 2)
                                full = xt_ps[:, :, :] if one else x_full[:, b, s, :, :]
                                nc.vector.tensor_tensor(x_low[:, b, s, :, :], full, x_high[:, b, s, :, :].bitcast(f32), ALU.subtract).then_inc(ready, 1)

                        for b in range(2):
                            lows(b, b, True)
                        chain = Chain(dve, s_dve)

                        def step(i, first, last):
                            chain.step(i)
                            for b in range(2):
                                g = 2 * i + b
                                for m in range(KD):
                                    dve.wait_ge(yz_ready, 2 * g + m + 1)
                                    chain.mark(nc.vector.tensor_tensor_scan(top[:, b, m, :], mask[:, bass.ds(g * GE, GE)], y_ps[m][:, :],
                                                                            top[:, 1 - b, m, GE - 1:GE], ALU.add, ALU.max))
                                    if not first:
                                        dve.wait_ge(agg_ready, 2 * g - 3 + m)
                                    chain.after()
                                    nc.vector.tensor_tensor(summ[:, b, m, :], z_ps[m][:, :], top[:, b, m, :], ALU.add).then_inc(sum_ready, 1)
                                if not last:
                                    lows(g + 2, b, False)
                                if not more:
                                    pass
                                elif b == 1:
                                    dve.wait_ge(row_turned, g)
                                    if not first:
                                        dve.wait_ge(row_out[0], 16 * i)
                                    nc.vector.tensor_copy(rows[:, 0, :, :], row_ps[:, :, :]).then_inc(row_ready, 1)
                                elif not first:
                                    dve.wait_ge(row_turned, g)
                                    if not (isinstance(i, int) and i < 2):
                                        dve.wait_ge(row_out[1], 16 * (i - 1))
                                    nc.vector.tensor_copy(rows[:, 1, :, :], row_ps[:, :, :]).then_inc(row_ready, 1)
                        loop(dve, STEPS, step, peeled=2)
                        if more:
                            dve.wait_ge(row_turned, NG)
                            dve.wait_ge(row_out[1], 16 * (STEPS - 1))
                            nc.vector.tensor_copy(rows[:, 1, :, :], row_ps[:, :, :]).then_inc(row_ready, 1)

                        dve.wait_ge(sq_ready, 2 * NG)
                        base_count = chain.base + chain.count
                        n = [base_count]

                        def link(ins):
                            n[0] += 1
                            ins.then_inc(s_dve, 1)
                            dve.wait_ge(s_dve, n[0])

                        for s in range(2):
                            link(nc.vector.tensor_reduce(stat[:, s, :], sums[:, s, :, :], AX_X, ALU.add))
                        link(nc.vector.tensor_scalar(stat[:, 0:2, :], stat[:, 0:2, :], 1.0 / N, None, ALU.mult))
                        link(nc.vector.tensor_tensor(stat[:, 2, :], stat[:, 0, :], stat[:, 0, :], ALU.mult))
                        link(nc.vector.tensor_tensor(stat[:, 2, :], stat[:, 1, :], stat[:, 2, :], ALU.subtract))
                        nc.vector.tensor_scalar(stat[:, 2, :], stat[:, 2, :], 0.0, EPS, ALU.max, ALU.add).then_inc(var_ready, 1)
                        dve.wait_ge(sd_ready, layer + 1)
                        link(nc.vector.reciprocal(stat[:, 4, :], stat[:, 3, :]))
                        link(nc.vector.tensor_tensor(bn_a[:], stat[:, 4, :], gam[:, :, layer], ALU.mult))
                        link(nc.vector.tensor_tensor(stat[:, 5, :], stat[:, 0, :], bn_a[:], ALU.mult))
                        nc.vector.tensor_tensor(bn_b[:], bet[:, :, layer], stat[:, 5, :], ALU.subtract)

        layering.close()

        with ExitStack() as ctx:
            spread = sb("spread", [P, 2, KD, P], f32, ctx)
            base_row = sb("base_row", [P, 2, D], f32, ctx)
            base_part = sb("base_part", [P, 3, 2, D], bf16, ctx)
            base_left = sb("base_left", [P, 2, 2, D], f32, ctx)
            base3 = sb("base3", [P, 2, D], bf16, ctx)
            xin = sb("xin", [P, 4, R, D], f32, ctx)
            xout = sb("xout", [P, 4, R, D], f32, ctx)
            own = sb("own_f", [P, 2, KD, GE], f32, ctx)
            act_cols = sb("act_cols", [P, 2, KD, GE], f32, ctx)
            xs = sb("xs", [P, 2, G, D], f32, ctx)
            yf = sb("yf", [P, 2, G, D], f32, ctx)
            idx = sb("idx_f", [P, 2, G], i32, ctx)
            work = {}
            for kind, rows_ in (("b", R), ("f", G)):
                work[kind] = (sb("bstats" + kind, [P, 2, rows_, 6], f32, ctx), sb("aggr" + kind, [P, 2, rows_, 2], f32, ctx),
                              sb("sd" + kind, [P, 2, rows_], f32, ctx), sb("rstd" + kind, [P, 2, rows_], f32, ctx),
                              sb("shift" + kind, [P, 2, rows_], f32, ctx))
            sum_ps = [pb(f"sum_ps{s}", [P, R, D], f32, ctx) for s in range(2)]
            fin_ps = pb("fin_ps", [P, G, D], f32, ctx)
            names = ("spread_ready", "spread_turned", "base_ready", "s_dve", "added_b", "added_f", "aggr_b", "aggr_f", "sd_b", "sd_f",
                     "norm_b", "norm_f", "y_b", "y_f", "act_ready", "idx_ready")
            (spread_ready, spread_turned, base_ready, s_dve, added_b, added_f, aggr_b, aggr_f, sd_b, sd_f,
             norm_b, norm_f, y_b, y_f, act_ready, idx_ready) = [whole.enter_context(nc.semaphore(n + "_o")) for n in names]
            x_in, out_done = [[whole.enter_context(nc.semaphore(f"{n}{k}")) for k in range(4)] for n in ("x_in", "out_done")]
            own_in, xs_in, done_out = [[whole.enter_context(nc.semaphore(f"{n}{b}_o")) for b in range(2)]
                                       for n in ("own_in", "xs_in", "done_out")]
            x_blocks = x[0:BLOCKS * BLOCK_ROWS, :].rearrange("(n p r) d -> n p (r d)", p=P, r=R)
            out_blocks = out[0:BLOCKS * BLOCK_ROWS, :].rearrange("(n p r) d -> n p (r d)", p=P, r=R)
            tail = [(P, R)] * (BLOCKS - 4 * BLOCK_STEPS) + ([(REST // RR, RR)] if REST else [])

            def stages(engine, step, tail_step):
                step(0, True, False, True, True)
                with engine.Fori(1, STEPS - 1) as i:
                    step(i, False, False, True, True)
                step(STEPS - 1, False, False, True, False)
                if BLOCK_STEPS - 1 > STEPS:
                    with engine.Fori(STEPS, BLOCK_STEPS - 1) as i:
                        step(i, False, False, False, False)
                step(BLOCK_STEPS - 1, False, True, False, False)
                for k in range(len(tail)):
                    tail_step(k)

            with nc.Block() as block:
                @block.sync
                def _(sp):
                    def load(i, k, np_=P, r_=R):
                        if np_ == P and r_ == R:
                            from_ = x_blocks[bass.ds(4 * i + k, 1), :, :].rearrange("a p f -> p (a f)")
                        else:
                            from_ = x[N - REST:N, :].rearrange("(p r) d -> p (r d)", r=RR)
                        sp.dma_start(xin[0:np_, k, 0:r_, :].rearrange("p r d -> p (r d)"), from_).then_inc(x_in[k], 16)

                    def load_own(g, b):
                        sp.dma_start(own[:, b, :, :].rearrange("p k f -> p (k f)"),
                                     agg_cols[LAYERS - 1][bass.ds(g, 1), :, :].rearrange("a p f -> p (a f)")).then_inc(own_in[b], 16)

                    def store(i, k, np_=P, r_=R):
                        sp.wait_ge(y_b, 4 * i + k + 1)
                        if np_ == P and r_ == R:
                            to = out_blocks[bass.ds(4 * i + k, 1), :, :].rearrange("a p f -> p (a f)")
                        else:
                            to = out[N - REST:N, :].rearrange("(p r) d -> p (r d)", r=RR)
                        sp.dma_start(to, xout[0:np_, k, 0:r_, :].rearrange("p r d -> p (r d)")).then_inc(out_done[k], 16)

                    for b in range(2):
                        load_own(b, b)
                    for k in range(4):
                        load(0, k)

                    def step(i, first, last, edges, ahead):
                        for k in range(4):
                            if not last:
                                sp.wait_ge(added_b, 4 * i + k + 1)
                                load(i + 1, k)
                            elif k < len(tail):
                                sp.wait_ge(added_b, 4 * i + k + 1)
                                load(i + 1, k, *tail[k])
                            store(i, k)
                            if k % 2 and edges:
                                b = k // 2
                                g = 2 * i + b
                                if ahead:
                                    sp.wait_ge(act_ready, g + 1)
                                    load_own(g + 2, b)
                                sp.wait_ge(y_f, g + 1)
                                sp.dma_start(done_rows[bass.ds(g * GE, GE), :].rearrange("(a p) d -> p a d", p=P), yf[:, b, :, :]).then_inc(done_out[b], 16)
                    stages(sp, step, lambda k: store(BLOCK_STEPS, k, *tail[k]))
                    for k in range(4):
                        sp.wait_ge(out_done[k], 16 * (BLOCK_STEPS + (k < len(tail))))
                    for b in range(2):
                        sp.wait_ge(done_out[b], 16 * STEPS)

                @block.gpsimd
                def _(pool):
                    def step(i, first, last):
                        for b in range(2):
                            g = 2 * i + b
                            if not first:
                                pool.wait_ge(added_f, g - 1)
                                pool.nop(nofuse=True)
                            nc.gpsimd.tensor_copy(idx[:, b, :], gat_src[:, bass.ds(G * g, G)]).then_inc(idx_ready, 1)
                            pool.wait_ge(idx_ready, g + 1)
                            pool.nop(nofuse=True)
                            for j in range(G):
                                nc.gpsimd.indirect_dma_start(xs[:, b, j, :], None, x[:, :],
                                                             bass.IndirectOffsetOnAxis(ap=idx[:, b, j:j + 1], axis=0)).then_inc(xs_in[b], 16)
                    loop(pool, STEPS, step)

                @block.tensor
                def _(pe):
                    pe.wait_ge(spread_ready, 1)
                    for k in range(KD):
                        ins = nc.tensor.matmul(fin_ps[:, 0, k * P:(k + 1) * P], spread[:, 1, k, :], ident[:], start=True, stop=True)
                    ins.then_inc(spread_turned, 1)
                    pe.wait_ge(base_ready, 1)

                    def add_block(i, k, np_, r_, start):
                        n = 4 * i + k
                        pe.wait_ge(x_in[k], 16 * i + 16)
                        if not start:
                            pe.wait_ge(y_b, n - 1)
                        for q in range(0, r_, 2):
                            to = sum_ps[k % 2][0:np_, q:q + 2, :].rearrange("p r d -> p (r d)")
                            nc.tensor.matmul(to, ident[0:np_, 0:np_], xin[0:np_, k, q:q + 2, :].rearrange("p r d -> p (r d)"), start=True, stop=False)
                            ins = nc.tensor.matmul(to, ones_bf[0:3, 0:np_], base3[0:3, :, :].rearrange("p r d -> p (r d)"), start=False, stop=True)
                        ins.then_inc(added_b, 1)

                    def add_group(i, b, start):
                        g = 2 * i + b
                        pe.wait_ge(xs_in[b], 64 * i + 64)
                        pe.wait_ge(act_ready, g + 1)
                        if not start:
                            pe.wait_ge(y_f, g)
                        for q in range(0, G, 2):
                            nc.tensor.matmul(fin_ps[:, q:q + 2, :].rearrange("p r d -> p (r d)"), ident[:],
                                             xs[:, b, q:q + 2, :].rearrange("p r d -> p (r d)"), start=True, stop=False)
                            for j in (q, q + 1):
                                for k in range(KD):
                                    ins = nc.tensor.matmul(fin_ps[:, j, k * P:(k + 1) * P], act_cols[:, b, k, j * P:(j + 1) * P], ident[:],
                                                           start=False, stop=(j == q + 1 and k == KD - 1))
                        ins.then_inc(added_f, 1)

                    def step(i, first, last, edges, ahead):
                        for k in range(4):
                            add_block(i, k, P, R, first and k < 2)
                            if k % 2 and edges:
                                add_group(i, k // 2, first and k == 1)
                    stages(pe, step, lambda k: add_block(BLOCK_STEPS, k, *tail[k], False))

                @block.vector
                def _(dve):
                    chain = Chain(dve, s_dve)

                    def link(ins):
                        chain.mark(ins)
                        chain.after()

                    for k in range(KD):
                        ins = nc.vector.tensor_scalar(spread[:, 1, k, :], ones[:], bn_b[:, k:k + 1], None, ALU.mult)
                    ins.then_inc(spread_ready, 1)
                    dve.wait_ge(spread_turned, 1)
                    for r in range(2):
                        link(nc.vector.tensor_scalar(base_row[:, r, :], fin_ps[:, 0, :], 0.0, None, ALU.max))
                    link(nc.vector.tensor_copy(base_part[:, 0, :, :], base_row[:]))
                    link(nc.vector.tensor_tensor(base_left[:, 0, :, :], base_row[:], base_part[:, 0, :, :], ALU.subtract))
                    link(nc.vector.tensor_copy(base_part[:, 1, :, :], base_left[:, 0, :, :]))
                    link(nc.vector.tensor_tensor(base_left[:, 1, :, :], base_left[:, 0, :, :], base_part[:, 1, :, :], ALU.subtract))
                    link(nc.vector.tensor_copy(base_part[:, 2, :, :], base_left[:, 1, :, :]))
                    link(nc.vector.tensor_scalar(base3[:], base_part[:, 0, :, :], ident[:, 0:1], None, ALU.mult))
                    link(nc.vector.scalar_tensor_tensor(base3[:], base_part[:, 1, :, :], ident[:, 1:2], base3[:], ALU.mult, ALU.add))
                    nc.vector.scalar_tensor_tensor(base3[:], base_part[:, 2, :, :], ident[:, 2:3], base3[:], ALU.mult, ALU.add).then_inc(base_ready, 1)
                    set_up = chain.count

                    links = [0]
                    s_links = [None]

                    def factors(kind, n, s, ps, added, aggr_, sd_, y_, norm_, np_, r_, base):
                        bstats, aggr, sd, rstd, shift = work[kind]
                        dve.wait_ge(added, n + 1)
                        for r in range(r_):
                            ins = nc.vector.bn_stats(bstats[0:np_, s, r, :], ps[0:np_, r, :])
                        chain.mark(ins)
                        chain.after()
                        dve.nop(nofuse=True)
                        for r in range(r_):
                            ins = nc.vector.bn_aggr(aggr[0:np_, s, r, :], bstats[0:np_, s, r, :])
                        chain.mark(ins)
                        chain.after()
                        nc.vector.tensor_scalar(sd[0:np_, s, 0:r_], aggr[0:np_, s, 0:r_, 1], EPS, None, ALU.add).then_inc(aggr_, 1)
                        dve.wait_ge(sd_, n + 1)
                        if base:
                            dve.wait_ge(y_, n - 1)
                        chain.mark(nc.vector.reciprocal(rstd[0:np_, s, 0:r_], sd[0:np_, s, 0:r_]))
                        chain.after()
                        nc.vector.scalar_tensor_tensor(shift[0:np_, s, 0:r_], aggr[0:np_, s, 0:r_, 0], -1.0, rstd[0:np_, s, 0:r_],
                                                       ALU.mult, ALU.mult).then_inc(norm_, 1)

                    def of_block(i, k, np_, r_, start):
                        factors("b", 4 * i + k, k % 2, sum_ps[k % 2], added_b, aggr_b, sd_b, y_b, norm_b, np_, r_, not start)

                    def of_group(i, b, start):
                        factors("f", 2 * i + b, b, fin_ps, added_f, aggr_f, sd_f, y_f, norm_f, P, G, not start)

                    MARKS = 3

                    def step(i, first, last, edges, ahead):
                        chain.base = set_up + MARKS * (6 * i if edges else 6 * STEPS + 4 * (i - STEPS))
                        chain.count = 0
                        for k in range(4):
                            of_block(i, k, P, R, first and k < 2)
                            if k % 2 and edges:
                                of_group(i, k // 2, first)

                    def tail_step(k):
                        chain.base, chain.count = set_up + MARKS * (6 * STEPS + 4 * (BLOCK_STEPS - STEPS) + k), 0
                        of_block(BLOCK_STEPS, k, *tail[k], False)
                    stages(dve, step, tail_step)

                @block.scalar
                def _(act):
                    def normalise(kind, n, s, ps, to, aggr_, sd_, norm_, y_, np_, r_, freed):
                        _, _, sd, rstd, shift = work[kind]
                        act.wait_ge(aggr_, n + 1)
                        nc.scalar.activation(sd[0:np_, s, 0:r_], sd[0:np_, s, 0:r_], ACT.Sqrt).then_inc(sd_, 1)
                        if freed:
                            act.wait_ge(*freed)
                        act.wait_ge(norm_, n + 1)
                        for r in range(r_):
                            ins = nc.scalar.activation(to[0:np_, r, :], ps[0:np_, r, :], ACT.Identity,
                                                       bias=shift[0:np_, s, r:r + 1], scale=rstd[0:np_, s, r:r + 1])
                        ins.then_inc(y_, 1)

                    def activate(g, i, b):
                        act.wait_ge(own_in[b], 16 * i + 16)
                        for k in range(KD):
                            ins = nc.scalar.activation(act_cols[:, b, k, :], own[:, b, k, :], ACT.Relu, bias=bn_b[:, k:k + 1], scale=bn_a[:, k:k + 1])
                        ins.then_inc(act_ready, 1)

                    for b in range(2):
                        activate(b, 0, b)

                    def of_block(i, k, np_, r_):
                        n = 4 * i + k
                        freed = None if isinstance(i, int) and i == 0 else (out_done[k], 16 * i)
                        normalise("b", n, k % 2, sum_ps[k % 2], xout[:, k, :, :], aggr_b, sd_b, norm_b, y_b, np_, r_, freed)

                    def step(i, first, last, edges, ahead):
                        for k in range(4):
                            of_block(i, k, P, R)
                            if k % 2 and edges:
                                b = k // 2
                                g = 2 * i + b
                                normalise("f", g, b, fin_ps, yf[:, b, :, :], aggr_f, sd_f, norm_f, y_f, P, G, None if first else (done_out[b], 16 * i))
                                if ahead:
                                    activate(g + 2, i + 1, b)
                    stages(act, step, lambda k: of_block(BLOCK_STEPS, k, *tail[k]))

        with ExitStack() as ctx:
            SLOTS = 2
            yo = sb("yo", [P, SLOTS, G, D], f32, ctx)
            idx = sb("idx_p", [P, SLOTS, G], i32, ctx)
            idx_ready = whole.enter_context(nc.semaphore("idx_ready_p"))
            yo_in, put = [[whole.enter_context(nc.semaphore(f"{n}{b}_p")) for b in range(SLOTS)] for n in ("yo_in", "put")]
            with nc.Block() as block:
                @block.sync
                def _(sp):
                    def step(i, first, last):
                        for b in range(SLOTS):
                            g = SLOTS * i + b
                            if not first:
                                sp.wait_ge(put[b], 64 * i)
                                sp.nop(nofuse=True)
                                sp.wait_ge(yo_in[b], 16 * i)
                            sp.dma_start(yo[:, b, :, :], done_rows[bass.ds(g * GE, GE), :].rearrange("(a p) d -> p a d", p=P)).then_inc(yo_in[b], 16)
                    loop(sp, NG // SLOTS, step)

                @block.gpsimd
                def _(pool):
                    def step(i, first, last):
                        for b in range(SLOTS):
                            g = SLOTS * i + b
                            if not first:
                                pool.wait_ge(put[b], 64 * i)
                                pool.nop(nofuse=True)
                            nc.gpsimd.tensor_copy(idx[:, b, :], put_src[:, bass.ds(G * g, G)]).then_inc(idx_ready, 1)
                            pool.wait_ge(idx_ready, g + 1)
                            pool.wait_ge(yo_in[b], 16 * i + 16)
                            pool.nop(nofuse=True)
                            for j in range(G):
                                nc.gpsimd.indirect_dma_start(out[:, :], bass.IndirectOffsetOnAxis(ap=idx[:, b, j:j + 1], axis=0),
                                                             yo[:, b, j, :], None, bounds_check=N - 1, oob_is_err=False).then_inc(put[b], 16)
                    loop(pool, NG // SLOTS, step)
                    for b in range(SLOTS):
                        pool.wait_ge(put[b], 64 * (NG // SLOTS))
                        pool.nop(nofuse=True)


_INS = ['x', 'src', 'dst', 'L0_gnn_thetas', 'L0_gnn_phis', 'L0_gnn_gammas', 'L0_gnn_betas']


def kernel(**inputs):
    import numpy as _np
    import concourse.bacc as _bacc
    from concourse import mybir as _mybir
    from concourse.bass_utils import run_bass_kernel_spmd as _run

    nc = _bacc.Bacc("TRN2", target_bir_lowering=False, num_devices=1)
    arrays, args = {}, []
    for name in _INS:
        a = _np.ascontiguousarray(inputs[name])
        arrays[f"in_{name}_dram"] = a
        args.append(nc.dram_tensor(f"in_{name}_dram", a.shape, _mybir.dt.from_np(a.dtype), kind="ExternalInput").ap())
    args.append(nc.dram_tensor("out_0_dram", inputs['x'].shape, _mybir.dt.float32, kind="ExternalOutput").ap())
    gnn_program(nc, *args)
    r = _run(nc, [arrays], core_ids=[0])
    return r.results[0]["out_0_dram"]
```

```python
import concourse.bass as bass
from concourse import mybir
from contextlib import ExitStack


def loop(engine, count, step, peeled=1):
    head = min(peeled, count - 1)
    for i in range(head):
        step(i, i == 0, False)
    if count - 1 > head:
        with engine.Fori(head, count - 1) as i:
            step(i, False, False)
    step(count - 1, count == 1, True)


class Chain:

    def __init__(self, engine, sem):
        self.engine, self.sem, self.base, self.count, self.per_step = engine, sem, 0, 0, None

    def step(self, i):
        if self.per_step is None and self.count:
            self.per_step = self.count
        self.base = 0 if self.per_step is None else i * self.per_step
        self.count = 0

    def mark(self, instruction):
        self.count += 1
        instruction.then_inc(self.sem, 1)

    def after(self):
        self.engine.wait_ge(self.sem, self.base + self.count)


def gnn_program(nc, x, src, dst, thetas, phis, gammas, betas, out):
    f32, i32 = mybir.dt.float32, mybir.dt.int32
    f16, bf16, f32r = mybir.dt.float16, mybir.dt.bfloat16, mybir.dt.float32r
    ALU = mybir.AluOpType
    ACT = mybir.ActivationFunctionType
    AX_X = mybir.AxisListType.X

    P = 128
    N, D = x.shape
    E = src.shape[0]
    LAYERS = thetas.shape[0]
    KD = D // P
    EPS = 1e-5
    EP = -(-E // 1024) * 1024
    NT = EP // P
    TC = NT // 2
    G = 4
    GE = G * P
    STEPS = EP // (2 * GE)
    NG = 2 * STEPS
    LOW = 512
    LOW_BITS = 9
    HC = -(-(N + 1) // (2 * LOW))
    HIGHS = 2 * HC
    PAD_KEY = N
    ABSENT = EP
    START_PENALTY = -2e38
    END_PENALTY = -1e30
    SKIP = float(1 << 20)
    assert HC <= P and TC <= P and D == KD * P and N < (1 << 20)

    BY_DVE = 2

    R = 6
    BLOCK_ROWS = P * R
    PAIRS = R // 2
    BLOCKS = N // BLOCK_ROWS
    BLOCK_STEPS = BLOCKS // 4
    REST = N - BLOCKS * BLOCK_ROWS
    RR = max((r for r in range(2, R + 1, 2) if REST % r == 0 and REST // r <= P), default=0)
    assert (REST == 0 or RR) and STEPS > 6 and BLOCK_STEPS > STEPS

    src_row = nc.dram_tensor("src_row", (EP,), f32).ap()
    high_row = nc.dram_tensor("high_row", (EP,), f32).ap()
    position_table = nc.dram_tensor("position_table", (HIGHS * LOW, 1), i32).ap()
    sorted_meta = nc.dram_tensor("sorted_meta", (EP, 2), i32).ap()
    sorted_row = nc.dram_tensor("sorted_row", (EP + 2,), f32).ap()
    start_row = nc.dram_tensor("start_row", (EP,), bf16).ap()
    end_row = nc.dram_tensor("end_row", (EP,), bf16).ap()
    agg_rows = [nc.dram_tensor(f"agg_rows{l}", (EP + 1, D), f32).ap() for l in range(LAYERS - 1)]
    agg_cols = [nc.dram_tensor(f"agg_cols{l}", (NG, P, KD * GE), f32).ap() for l in range(LAYERS)]
    done_rows = nc.dram_tensor("done_rows", (EP, D), f32).ap()

    whole = ExitStack()
    with whole:
        def sb(name, shape, dt, ctx=whole):
            return ctx.enter_context(nc.sbuf_tensor(name, shape, dt))

        def pb(name, shape, dt, ctx=whole):
            return ctx.enter_context(nc.psum_tensor(name, shape, dt))

        sort_signals, sorting_done = [], ExitStack()

        def signal(name):
            sort_signals.append(sorting_done.enter_context(nc.semaphore(name)))
            return sort_signals[-1]

        ident = sb("ident", [P, P], f32)
        ones = sb("ones", [P, P], f32)
        ones_bf = sb("ones_bf", [3, P], bf16)
        gat_src = sb("gat_src", [P, NT], i32)
        gat_dst = sb("gat_dst", [P, NT], i32)
        ask = sb("ask", [P, 2, G], i32)
        told = sb("told", [P, 2, G], i32)
        gat_pos = sb("gat_pos", [P, NT], i32)
        put_src = sb("put_src", [P, NT], i32)
        bn_a = sb("bn_a", [P, KD], f32)
        bn_b = sb("bn_b", [P, KD], f32)
        gam = sb("gam", [P, KD, LAYERS], f32)
        bet = sb("bet", [P, KD, LAYERS], f32)

        sorting = ExitStack()
        with sorting:
            src_col = sb("src_col", [P, NT], f32, sorting)
            low_col = sb("low_col", [P, NT], f32, sorting)
            minus_low = sb("minus_low", [P, NT], f32, sorting)
            high_col = sb("high_col", [P, NT], f32, sorting)
            meta = sb("meta", [P, NT, 2], i32, sorting)
            iota_low = sb("iota_low", [P, LOW], f16, sorting)
            iota_high = sb("iota_high", [P, HIGHS], f16, sorting)
            minus_part = sb("minus_part", [P, 2], f32, sorting)
            earlier = sb("earlier", [P, GE], f16, sorting)
            below = sb("below", [P, P], f32, sorting)
            first_pos = sb("first_pos", [HC, 2, LOW], f32, sorting)
            counts = [pb(f"counts{c}", [HC, LOW], f32, sorting) for c in range(2)]

            with ExitStack() as ctx:
                raw = sb("raw", [TC, 2, 2, P], i32, ctx)
                rawf = sb("rawf", [TC, 2, 2, P], f32, ctx)
                high_i = sb("high_i", [TC, 2, P], i32, ctx)
                high_f = sb("high_f", [TC, 2, P], f32, ctx)
                col_i = sb("col_i", [P, 3, NT], i32, ctx)
                zrow = sb("zrow", [1, D], f32, ctx)
                tp = [pb(f"tp{s}", [P, NT], f32, ctx) for s in range(2)]
                s_fill = signal("s_fill")
                s_raw = whole.enter_context(nc.semaphore("s_raw"))
                s_const = signal("s_const")
                s_pool = signal("s_pool")
                s_rawf = signal("s_rawf")
                s_tp = signal("s_tp")
                s_dve = signal("s_dve")
                s_out = whole.enter_context(nc.semaphore("s_out"))
                s_high = signal("s_high")
                loads = [0]
                with nc.Block() as block:
                    @block.sync
                    def _(sp):
                        sp.wait_ge(s_fill, 1)
                        for which, edges in enumerate((src, dst)):
                            for c in range(2):
                                full = max(min(E // P - c * TC, TC), 0)
                                if full:
                                    sp.dma_start(raw[0:full, which, c, :], edges[c * TC * P:(c * TC + full) * P]
                                                 .rearrange("(t p) -> t p", p=P)).then_inc(s_raw, 16)
                                    loads[0] += 16
                                if full < TC and E % P and full == E // P - c * TC:
                                    sp.dma_start(raw[full:full + 1, which, c, 0:E % P],
                                                 edges[E - E % P:E].unsqueeze(0)).then_inc(s_raw, 16)
                                    loads[0] += 16
                        with nc.allow_non_contiguous_dma(reason="small, once"):
                            for k in range(KD):
                                for l in range(LAYERS):
                                    sp.dma_start(gam[:, k, l:l + 1], gammas[l, k * P:(k + 1) * P].unsqueeze(1)).then_inc(s_out, 16)
                                    sp.dma_start(bet[:, k, l:l + 1], betas[l, k * P:(k + 1) * P].unsqueeze(1)).then_inc(s_out, 16)
                        sp.wait_ge(s_rawf, 1)
                        sp.dma_start(src_row.rearrange("(c t p) -> t c p", c=2, p=P), rawf[:, 0, :, :]).then_inc(s_out, 16)
                        sp.wait_ge(s_high, 1)
                        sp.dma_start(high_row.rearrange("(c t p) -> t c p", c=2, p=P), high_f[:, :, :]).then_inc(s_out, 16)
                        sp.wait_ge(s_const, 1)
                        for l in range(LAYERS - 1):
                            sp.dma_start(agg_rows[l][ABSENT:ABSENT + 1, :], zrow[:, :]).then_inc(s_out, 16)
                        sp.wait_ge(s_out, 16 * (2 * KD * LAYERS + 2 + LAYERS - 1))

                    @block.gpsimd
                    def _(pool):
                        chain = Chain(pool, s_pool)
                        nc.gpsimd.memset(raw[:, 1, :, :], 0)
                        nc.gpsimd.memset(raw[:, 0, :, :], PAD_KEY).then_inc(s_fill, 1)
                        nc.gpsimd.memset(zrow[:], 0.0)
                        nc.gpsimd.memset(ones_bf[:], 1.0)
                        nc.gpsimd.memset(ones[:], 1.0)
                        nc.gpsimd.memset(ident[:], 0.0)
                        nc.gpsimd.memset(below[:], 1.0)
                        chain.mark(nc.gpsimd.memset(earlier[:], 1.0))
                        chain.after()
                        nc.gpsimd.affine_select(out=ident[:], in_=ident[:], compare_op=ALU.not_equal, fill=1.0, base=0,
                                                pattern=[[1, P]], channel_multiplier=-1)
                        nc.gpsimd.affine_select(out=below[:], in_=below[:], compare_op=ALU.is_gt, fill=0.0, base=0,
                                                pattern=[[1, P]], channel_multiplier=-1)
                        nc.gpsimd.affine_select(out=earlier[:, GE - P:GE], in_=earlier[:, GE - P:GE], compare_op=ALU.is_gt,
                                                fill=0.0, base=0, pattern=[[-1, P]], channel_multiplier=1)
                        nc.gpsimd.iota(iota_low[:], [[1, LOW]], base=0, channel_multiplier=0, allow_small_or_imprecise_dtypes=True)
                        nc.gpsimd.iota(iota_high[:], [[1, HIGHS]], base=0, channel_multiplier=0, allow_small_or_imprecise_dtypes=True)
                        nc.gpsimd.iota(minus_part[:], [[-HC, 2]], base=0, channel_multiplier=-1,
                                       allow_small_or_imprecise_dtypes=True).then_inc(s_const, 1)

                    @block.vector
                    def _(dve):
                        chain = Chain(dve, s_dve)
                        dve.wait_ge(s_raw, loads[0])
                        nc.vector.tensor_copy(rawf[:], raw[:]).then_inc(s_rawf, 1)
                        chain.mark(nc.vector.tensor_single_scalar(high_i[:], raw[:, 0, :, :], LOW_BITS, ALU.logical_shift_right))
                        chain.after()
                        nc.vector.tensor_copy(high_f[:], high_i[:]).then_inc(s_high, 1)
                        dve.wait_ge(s_tp, 1)
                        nc.vector.tensor_copy(src_col[:], tp[0][:, :])
                        nc.vector.tensor_copy(meta[:, :, 0], tp[0][:, :])
                        nc.vector.tensor_copy(meta[:, :, 1], tp[1][:, :])
                        chain.mark(nc.vector.tensor_copy(col_i[:, 0, :], tp[0][:, :]))
                        chain.after()
                        nc.vector.tensor_single_scalar(col_i[:, 1, :], col_i[:, 0, :], LOW_BITS, ALU.logical_shift_right)
                        chain.mark(nc.vector.tensor_single_scalar(col_i[:, 2, :], col_i[:, 0, :], LOW - 1, ALU.bitwise_and))
                        chain.after()
                        nc.vector.tensor_copy(high_col[:], col_i[:, 1, :])
                        nc.vector.tensor_copy(low_col[:], col_i[:, 2, :])
                        nc.vector.tensor_scalar(minus_low[:], col_i[:, 2, :], -1.0, None, ALU.mult)

                    @block.tensor
                    def _(pe):
                        pe.wait_ge(s_const, 1)
                        pe.wait_ge(s_rawf, 1)
                        for which in range(2):
                            for c in range(2):
                                last = nc.tensor.transpose(tp[which][:, c * TC:(c + 1) * TC], rawf[:, which, c, :], ident[0:TC, 0:TC])
                        last.then_inc(s_tp, 1)

            with ExitStack() as ctx:
                hot_high = sb("hot_high", [P, 2, G, HIGHS], f16, ctx)
                hot_low = sb("hot_low", [P, 2, G, LOW], f16, ctx)
                incl = sb("incl", [HC, 2, LOW], f32, ctx)
                cnt = sb("cnt", [HC, 2, LOW], f32, ctx)
                ones_low = sb("ones_low", [HC, LOW], f32, ctx)
                base = sb("base", [HC, 2], f32, ctx)
                table = sb("table", [HC, 2, LOW], i32, ctx)
                base_ps = pb("base_ps", [HC, 2], f32, ctx)
                hot_ready = signal("hot_ready")
                hot_used = signal("hot_used")
                s_tot = signal("s_tot")
                s_base = signal("s_base")
                s_dve = signal("s_dve2")
                s_table = signal("s_table")
                s_stored = whole.enter_context(nc.semaphore("s_stored"))
                with nc.Block() as block:
                    @block.vector
                    def _(dve):
                        def step(i, first, last):
                            for b in range(2):
                                g = 2 * i + b
                                if not first:
                                    dve.wait_ge(hot_used, g - 1)
                                for j in range(G):
                                    t = G * g + j
                                    nc.vector.tensor_scalar(hot_high[:, b, j, :], iota_high[:], high_col[:, bass.ds(t, 1)], None, ALU.is_equal)
                                    ins = nc.vector.tensor_scalar(hot_low[:, b, j, :], iota_low[:], low_col[:, bass.ds(t, 1)], None, ALU.is_equal)
                                ins.then_inc(hot_ready, 1)
                        loop(dve, STEPS, step)

                        chain = Chain(dve, s_dve)
                        nc.vector.memset(ones_low[:], 1.0)
                        dve.wait_ge(hot_used, NG)
                        for c in range(2):
                            chain.mark(nc.vector.tensor_copy(cnt[:, c, :], counts[c][:, :]))
                        chain.after()
                        for c in range(2):
                            ins = nc.vector.tensor_tensor_scan(incl[:, c, :], ones_low[:], cnt[:, c, :], 0.0, ALU.mult, ALU.add)
                        ins.then_inc(s_tot, 1)
                        dve.wait_ge(s_base, 1)
                        chain.mark(nc.vector.tensor_copy(base[:], base_ps[:]))
                        chain.after()
                        for c in range(2):
                            chain.mark(nc.vector.tensor_scalar(incl[:, c, :], incl[:, c, :], base[:, c:c + 1], None, ALU.add))
                        chain.after()
                        chain.mark(nc.vector.tensor_tensor(first_pos[:], incl[:], cnt[:], ALU.subtract))
                        chain.after()
                        chain.mark(nc.vector.tensor_scalar(incl[:], incl[:], -1.0 - ABSENT, None, ALU.add))
                        chain.after()
                        chain.mark(nc.vector.scalar_tensor_tensor(cnt[:], cnt[:], 0.0, incl[:], ALU.is_gt, ALU.mult))
                        chain.after()
                        nc.vector.tensor_scalar(table[:], cnt[:], float(ABSENT), None, ALU.add).then_inc(s_table, 1)

                    @block.tensor
                    def _(pe):
                        def step(i, first, last):
                            for b in range(2):
                                g = 2 * i + b
                                pe.wait_ge(hot_ready, g + 1)
                                for j in range(G):
                                    for c in range(2):
                                        ins = nc.tensor.matmul(counts[c][:, :], hot_high[:, b, j, c * HC:(c + 1) * HC], hot_low[:, b, j, :],
                                                               start=(first and b == 0 and j == 0), stop=(last and b == 1 and j == G - 1),
                                                               skip_group_check=True)
                                ins.then_inc(hot_used, 1)
                        loop(pe, STEPS, step)
                        pe.wait_ge(s_tot, 1)
                        nc.tensor.matmul(base_ps[:, 0:1], below[0:HC, 0:HC], incl[:, 0, LOW - 1:LOW], start=True, stop=True)
                        nc.tensor.matmul(base_ps[:, 1:2], below[0:HC, 0:HC], incl[:, 1, LOW - 1:LOW], start=True, stop=False)
                        nc.tensor.matmul(base_ps[:, 1:2], ones[0:HC, 0:HC], incl[:, 0, LOW - 1:LOW], start=False, stop=True).then_inc(s_base, 1)

                    @block.sync
                    def _(sp):
                        sp.wait_ge(s_table, 1)
                        sp.dma_start(position_table.rearrange("(c h l) o -> h c (l o)", c=2, l=LOW), table[:]).then_inc(s_stored, 16)
                        sp.wait_ge(s_stored, 16)

            with ExitStack() as ctx:
                hot_high = sb("hot_high2", [P, 2, G, HIGHS], f16, ctx)
                hot_low = sb("hot_low2", [P, 2, G, LOW], f16, ctx)
                hot_rows = sb("hot_rows", [HC, 2, 2, GE], f16, ctx)
                keys = sb("keys", [P, 2, GE], f32, ctx)
                highs = sb("highs", [HC, 2, GE], f32, ctx)
                c_hi = sb("c_hi", [HC, 2, 2, LOW], f16, ctx)
                c_lo = sb("c_lo", [HC, 2, 2, LOW], f16, ctx)
                junk = sb("junk", [P, G, LOW], f16, ctx)
                junk2 = sb("junk2", [P, G, LOW], f16, ctx)
                same = sb("same", [P, 2, G], f32, ctx)
                before = sb("before", [P, 2, G], f32, ctx)
                pos = sb("pos", [P, 2, G], i32, ctx)
                row = sb("row", [P, 2, G, 2], i32, ctx)
                off_rows = sb("off_rows", [HC, 2, GE], f32, ctx)
                off_low = sb("off_low", [P, G - BY_DVE, LOW], f32, ctx)
                found = [pb(f"found{j}", [P, LOW], f32, ctx) for j in range(G)]
                names = ("hi_ready", "lo_ready", "rows_ready", "hot_ready2", "found_ready", "found_used", "next_ready",
                         "pos_ready", "keys_used", "low_ready", "s_act3")
                (hi_ready, lo_ready, rows_ready, hot_ready, found_ready, found_used, next_ready,
                 pos_ready, keys_used, low_ready, s_act) = [signal(n) for n in names]
                keys_in, highs_in = [[whole.enter_context(nc.semaphore(f"{n}{b}")) for b in range(2)] for n in ("keys_in", "highs_in")]
                scattered = [whole.enter_context(nc.semaphore(f"scattered{b}")) for b in range(2)]
                with nc.Block() as block:
                    @block.sync
                    def _(sp):
                        def step(i, first, last):
                            for b in range(2):
                                g = 2 * i + b
                                if not first:
                                    sp.wait_ge(rows_ready, g - 1)
                                sp.dma_start(highs[:, b, :], high_row[bass.ds(g * GE, GE)].partition_broadcast(HC)).then_inc(highs_in[b], 16)
                                if not first:
                                    sp.wait_ge(keys_used, g - 1)
                                sp.dma_start(keys[:, b, :], src_row[bass.ds(g * GE, GE)].partition_broadcast(P)).then_inc(keys_in[b], 16)
                        loop(sp, STEPS, step)

                    @block.scalar
                    def _(act):
                        chain = Chain(act, s_act)

                        def hots(g, i, b, start2):
                            act.wait_ge(highs_in[b], 16 * i + 16)
                            for c in range(2):
                                ins = nc.scalar.activation(off_rows[:, c, :], highs[:, b, :], ACT.Square, bias=minus_part[0:HC, c:c + 1])
                            chain.mark(ins)
                            for n in range(G - BY_DVE):
                                ins = nc.scalar.activation(off_low[:, n, :], iota_low[:], ACT.Square, bias=minus_low[:, bass.ds(G * g + BY_DVE + n, 1)])
                            chain.mark(ins)
                            chain.after()
                            if not start2:
                                act.wait_ge(found_ready, G * (g - 1))
                            nc.scalar.activation(hot_rows[:, b, :, :], off_rows[:, :, :], ACT.Relu, bias=ones[0:HC, 0:1], scale=-1.0).then_inc(rows_ready, 1)
                            if not start2:
                                act.wait_ge(next_ready, g)
                                act.wait_ge(found_used, G * (g - 1))
                            nc.scalar.activation(hot_low[:, b, BY_DVE:G, :], off_low[:, :, :], ACT.Relu, bias=ones[:, 0:1], scale=-1.0).then_inc(low_ready, 1)
                            act.wait_ge(rows_ready, g + 1)
                            act.wait_ge(low_ready, g + 1)

                        def step(i, first, last):
                            chain.base, chain.count = 2 + 4 * i, 0
                            for b in range(2):
                                g = 2 * i + b
                                act.wait_ge(next_ready, g + 1)
                                if not first:
                                    act.wait_ge(found_ready, G * (g - 1))
                                for c in range(2):
                                    ins = nc.scalar.copy(c_hi[:, b, c, :], counts[c][:, :])
                                ins.then_inc(hi_ready, 1)
                                if not (last and b == 1):
                                    hots(g + 1, i + b, 1 - b, first and b == 0)
                        hots(0, 0, 0, True)
                        loop(act, STEPS, step)

                    @block.tensor
                    def _(pe):
                        for c in range(2):
                            ins = nc.tensor.matmul(counts[c][:, :], ident[0:HC, 0:HC], first_pos[:, c, :], start=True, stop=False,
                                                   skip_group_check=True)
                        ins.then_inc(next_ready, 1)

                        def step(i, first, last):
                            for b in range(2):
                                g = 2 * i + b
                                pe.wait_ge(hi_ready, g + 1)
                                pe.wait_ge(lo_ready, g + 1)
                                pe.wait_ge(hot_ready, g + 1)
                                pe.wait_ge(low_ready, g + 1)
                                for j in range(G):
                                    for c in range(2):
                                        ins = nc.tensor.matmul(counts[c][:, :], hot_high[:, b, j, c * HC:(c + 1) * HC], hot_low[:, b, j, :],
                                                               start=False, stop=(last and b == 1 and j == G - 1), skip_group_check=True)
                                ins.then_inc(next_ready, 1)
                                pe.wait_ge(rows_ready, g + 1)
                                for j in range(G):
                                    if not (first and b == 0):
                                        pe.wait_ge(found_used, G * (g - 1) + j + 1)
                                    n = 0
                                    for c in range(2):
                                        for part in (c_hi, c_lo):
                                            ins = nc.tensor.matmul(found[j][:, :], hot_rows[:, b, c, j * P:(j + 1) * P], part[:, b, c, :],
                                                                   start=(n == 0), stop=(n == 3))
                                            n += 1
                                    ins.then_inc(found_ready, 1)
                        loop(pe, STEPS, step)

                    @block.vector
                    def _(dve):
                        def hots(g, b, start2):
                            if not start2:
                                dve.wait_ge(next_ready, g)
                            for j in range(G):
                                t = G * g + j
                                ins = nc.vector.tensor_scalar(hot_high[:, b, j, :], iota_high[:], high_col[:, bass.ds(t, 1)], None, ALU.is_equal)
                                if j < BY_DVE:
                                    ins = nc.vector.tensor_scalar(hot_low[:, b, j, :], iota_low[:], low_col[:, bass.ds(t, 1)], None, ALU.is_equal)
                            ins.then_inc(hot_ready, 1)

                        def place(behind, b):
                            dve.wait_ge(keys_used, behind)
                            dve.wait_ge(hot_ready, behind)
                            dve.wait_ge(low_ready, behind)
                            for j in range(G):
                                dve.wait_ge(found_ready, G * (behind - 1) + j + 1)
                                ins = nc.vector.scalar_tensor_tensor(junk2[:, j, :], found[j][:, :], 1.0, hot_low[:, b, j, :], ALU.mult, ALU.mult,
                                                                     accum_out=before[:, b, j:j + 1])
                                ins.then_inc(found_used, 1)
                            dve.wait_ge(found_used, G * behind)
                            nc.vector.tensor_tensor(pos[:, b, :], same[:, b, :], before[:, b, :], ALU.add).then_inc(pos_ready, 1)

                        def step(i, first, last):
                            for b in range(2):
                                g = 2 * i + b
                                dve.wait_ge(hi_ready, g + 1)
                                if not first:
                                    dve.wait_ge(found_ready, G * (g - 1))
                                for c in range(2):
                                    ins = nc.vector.tensor_tensor(c_lo[:, b, c, :], counts[c][:, :], c_hi[:, b, c, :], ALU.subtract)
                                ins.then_inc(lo_ready, 1)
                                if not (first and b == 0):
                                    place(g, 1 - b)
                                if not first:
                                    dve.wait_ge(scattered[b], 64 * i)
                                nc.vector.tensor_copy(row[:, b, :, :], meta[:, bass.ds(G * g, G), :])
                                dve.wait_ge(keys_in[b], 16 * i + 16)
                                for j in range(G):
                                    t = G * g + j
                                    wide = (j + 1) * P
                                    ins = nc.vector.scalar_tensor_tensor(junk[:, j, 0:wide], keys[:, b, 0:wide], src_col[:, bass.ds(t, 1)],
                                                                         earlier[:, GE - wide:GE], ALU.is_equal, ALU.mult,
                                                                         accum_out=same[:, b, j:j + 1])
                                ins.then_inc(keys_used, 1)
                                if not (last and b == 1):
                                    hots(g + 1, 1 - b, first and b == 0)
                        hots(0, 0, True)
                        loop(dve, STEPS, step)
                        place(NG, 1)

                    @block.gpsimd
                    def _(pool):
                        def step(i, first, last):
                            for b in range(2):
                                g = 2 * i + b
                                pool.wait_ge(pos_ready, g + 1)
                                pool.nop(nofuse=True)
                                for j in range(G):
                                    nc.gpsimd.indirect_dma_start(sorted_meta[:, :], bass.IndirectOffsetOnAxis(ap=pos[:, b, j:j + 1], axis=0),
                                                                 row[:, b, j, :], None).then_inc(scattered[b], 16)
                        loop(pool, STEPS, step)
                        for b in range(2):
                            pool.wait_ge(scattered[b], 64 * STEPS)
                            pool.nop(nofuse=True)

        IN_MASKS, AFTER_LAYER_0, IN_LAYER_1 = [min(n, (STEPS - 2) // 4) for n in (4, 2, 3)]
        LEAD = IN_MASKS + AFTER_LAYER_0 + IN_LAYER_1
        ask_ready, pos_kept, *pos_in = [whole.enter_context(nc.semaphore(n)) for n in ("ask_ready", "pos_kept", "pos_in0", "pos_in1")]

        def keep(i, b):
            nc.gpsimd.wait_ge(pos_in[b], 64 * i + 64)
            nc.gpsimd.tensor_copy(gat_pos[:, bass.ds(G * (2 * i + b), G)], told[:, b, :]).then_inc(pos_kept, 1)

        def look_up(i, start=False):
            for b in range(2):
                g = 2 * i + b
                if not start:
                    keep(i - 1, b)
                nc.gpsimd.tensor_copy(ask[:, b, :], gat_dst[:, bass.ds(G * g, G)]).then_inc(ask_ready, 1)
                nc.gpsimd.wait_ge(ask_ready, g + 1)
                if not start:
                    nc.gpsimd.wait_ge(pos_kept, g - 1)
                nc.gpsimd.nop(nofuse=True)
                for j in range(G):
                    nc.gpsimd.indirect_dma_start(told[:, b, j:j + 1], None, position_table[:, :],
                                                 bass.IndirectOffsetOnAxis(ap=ask[:, b, j:j + 1], axis=0)).then_inc(pos_in[b], 16)

        layering = ExitStack()
        mask = sb("mask", [P, EP], bf16, layering)

        with ExitStack() as ctx:
            sm = sb("sm", [TC, 2, P, 2], i32, ctx)
            here = sb("here", [TC, 2, P], f32, ctx)
            prev = sb("prev", [TC, 2, P], f32, ctx)
            nxt = sb("nxt", [TC, 2, P], f32, ctx)
            cols = sb("cols", [TC, 3, 2, P], f32, ctx)
            flag = sb("flag", [TC, 2, P], f32, ctx)
            pen = sb("pen", [TC, 2, 2, P], bf16, ctx)
            edge = sb("edge", [1, 2], f32, ctx)
            tp = [pb(f"tq{s}", [P, NT], f32, ctx) for s in range(3)]
            (here_ready, edge_ready, pens_ready, cols_ready, tp_ready, s_dve, dst_ready, dst_turned, dst_cols) = [
                signal(n) for n in ("here_ready", "edge_ready", "pens_ready", "cols_ready", "tp_ready", "s_dve4", "dst_ready", "dst_turned",
                                    "dst_cols")]
            m_in, row_out, shift_in, pens_out, mask_in = [whole.enter_context(nc.semaphore(n))
                                                          for n in ("m_in", "row_out", "shift_in", "pens_out", "mask_in")]
            with nc.Block() as block:
                @block.sync
                def _(sp):
                    sp.dma_start(sm[:].rearrange("t c p m -> t c (p m)"), sorted_meta.rearrange("(c t p) m -> t c (p m)", c=2, p=P)).then_inc(m_in, 16)
                    sp.wait_ge(edge_ready, 1)
                    sp.dma_start(sorted_row[0:1].unsqueeze(0), edge[:, 0:1]).then_inc(row_out, 16)
                    sp.dma_start(sorted_row[EP + 1:EP + 2].unsqueeze(0), edge[:, 1:2]).then_inc(row_out, 16)
                    sp.wait_ge(here_ready, 1)
                    sp.dma_start(sorted_row[1:EP + 1].rearrange("(c t p) -> t c p", c=2, p=P), here[:]).then_inc(row_out, 16)
                    sp.wait_ge(row_out, 48)
                    sp.dma_start(prev[:], sorted_row[0:EP].rearrange("(c t p) -> t c p", c=2, p=P)).then_inc(shift_in, 16)
                    sp.dma_start(nxt[:], sorted_row[2:EP + 2].rearrange("(c t p) -> t c p", c=2, p=P)).then_inc(shift_in, 16)
                    sp.wait_ge(pens_ready, 1)
                    sp.dma_start(start_row.rearrange("(c t p) -> t c p", c=2, p=P), pen[:, 0, :, :]).then_inc(pens_out, 16)
                    sp.dma_start(end_row.rearrange("(c t p) -> t c p", c=2, p=P), pen[:, 1, :, :]).then_inc(pens_out, 16)
                    sp.wait_ge(pens_out, 32)
                    sp.dma_start(mask[:], start_row.partition_broadcast(P)).then_inc(mask_in, 16)
                    sp.wait_ge(mask_in, 16)

                @block.vector
                def _(dve):
                    chain = Chain(dve, s_dve)
                    nc.vector.memset(edge[:, 0:1], -1.0)
                    nc.vector.memset(edge[:, 1:2], float(N + 1)).then_inc(edge_ready, 1)
                    dve.wait_ge(m_in, 16)
                    nc.vector.tensor_copy(here[:], sm[:, :, :, 0]).then_inc(here_ready, 1)
                    nc.vector.tensor_copy(cols[:, 1, :, :], sm[:, :, :, 1]).then_inc(dst_ready, 1)
                    dve.wait_ge(here_ready, 1)
                    nc.vector.tensor_scalar(cols[:, 0, :, :], here[:], float(N - 1), None, ALU.min)
                    dve.wait_ge(dst_turned, 1)
                    nc.vector.tensor_copy(gat_dst[:], tp[1][:, :]).then_inc(dst_cols, 1)
                    dve.wait_ge(shift_in, 32)
                    chain.mark(nc.vector.tensor_tensor(prev[:], here[:], prev[:], ALU.not_equal))
                    chain.mark(nc.vector.tensor_tensor(nxt[:], here[:], nxt[:], ALU.is_equal))
                    chain.after()
                    nc.vector.tensor_scalar(pen[:, 0, :, :], prev[:], START_PENALTY, None, ALU.mult)
                    chain.mark(nc.vector.scalar_tensor_tensor(flag[:], here[:], float(N), nxt[:], ALU.is_ge, ALU.max))
                    chain.after()
                    nc.vector.tensor_scalar(pen[:, 1, :, :], flag[:], END_PENALTY, None, ALU.mult).then_inc(pens_ready, 1)
                    nc.vector.scalar_tensor_tensor(cols[:, 2, :, :], flag[:], SKIP, here[:], ALU.mult, ALU.add).then_inc(cols_ready, 1)
                    dve.wait_ge(tp_ready, 2)
                    for s, to in ((0, gat_src), (2, put_src)):
                        nc.vector.tensor_copy(to[:], tp[s][:, :])

                @block.tensor
                def _(pe):
                    def turn(s, signal_):
                        for c in range(2):
                            ins = nc.tensor.transpose(tp[s][:, c * TC:(c + 1) * TC], cols[:, s, c, :], ident[0:TC, 0:TC])
                        ins.then_inc(signal_, 1)

                    pe.wait_ge(dst_ready, 1)
                    turn(1, dst_turned)
                    pe.wait_ge(cols_ready, 1)
                    turn(0, tp_ready)
                    turn(2, tp_ready)

                @block.gpsimd
                def _(pool):
                    pool.wait_ge(dst_cols, 1)
                    for i in range(IN_MASKS):
                        look_up(i, i == 0)

        with nc.Block() as block:
            @block.gpsimd
            def _(pool):
                for spent in sort_signals:
                    pool.sem_clear(spent)
        sorting_done.close()

        w_in, w_t, w_ev, sd_ready, var_ready = [whole.enter_context(nc.semaphore(n)) for n in
                                                ("w_in", "w_t", "w_ev", "sd_ready", "var_ready")]
        for layer in range(LAYERS):
            one = layer == 0
            more = layer < LAYERS - 1
            with ExitStack() as ctx:
                L = str(layer)
                w_raw = sb("w_raw" + L, [P, 2, KD, D], f32, ctx)
                w_full = sb("w_full" + L, [P, 2, KD, D], f32, ctx)
                w_high = sb("w_high" + L, [P, 2, KD, D], f32r, ctx)
                w_low = sb("w_low" + L, [P, 2, KD, D], f32r, ctx)
                fresh = sb("fresh" + L, [P, 2, G, D], f32, ctx)
                own = sb("own" + L, [P, 2, G, D], f32, ctx)
                idx = sb("idx" + L, [P, 2, 2, G], i32, ctx)
                pen = sb("pen" + L, [1, 2, GE], bf16, ctx)
                x_full = None if one else sb("x_full" + L, [P, 2, 2, KD, GE], f32, ctx)
                x_high = sb("x_high" + L, [P, 2, 2, KD, GE], f32r, ctx)
                x_low = sb("x_low" + L, [P, 2, 2, KD, GE], f32r, ctx)
                top = sb("top" + L, [P, 2, KD, GE], f32, ctx)
                summ = sb("summ" + L, [P, 2, KD, GE], f32, ctx)
                agg = sb("agg" + L, [P, 2, KD, GE], f32, ctx)
                sq = sb("sq" + L, [P, GE], f32, ctx)
                rows = sb("rows" + L, [P, 2, G, D], f32, ctx)
                sums = sb("sums" + L, [P, 2, KD, NG], f32, ctx)
                stat = sb("stat" + L, [P, 6, KD], f32, ctx)
                xt_ps = pb("xt_ps" + L, [P, KD, GE], f32, ctx)
                y_ps = [pb(f"y_ps{m}" + L, [P, GE], f32, ctx) for m in range(KD)]
                z_ps = [pb(f"z_ps{m}" + L, [P, GE], f32, ctx) for m in range(KD)]
                row_ps = pb("row_ps" + L, [P, G, D], f32, ctx)
                names = ["idx_ready", "j_turned", "j_high", "j_ready", "i_high", "i_ready", "yz_ready", "sum_ready",
                         "agg_ready", "sq_ready", "row_turned", "row_ready", "s_dve"] + (["i_turned"] if one else ["j_full", "i_full"])
                signals = [whole.enter_context(nc.semaphore(n + L)) for n in names]
                (idx_ready, j_turned, j_high, j_ready, i_high, i_ready, yz_ready, sum_ready,
                 agg_ready, sq_ready, row_turned, row_ready, s_dve) = signals[:13]
                i_turned, (j_full, i_full) = (signals[13], (None, None)) if one else (None, signals[13:])
                j_in, i_in, pen_in, agg_out, row_out = [[whole.enter_context(nc.semaphore(f"{n}{b}_{L}")) for b in range(2)]
                                                        for n in ("j_in", "i_in", "pen_in", "agg_out", "row_out")]
                with nc.Block() as block:
                    @block.gpsimd
                    def _(pool):
                        def gather(i, first, last):
                            for b in range(2):
                                g = 2 * i + b
                                if layer == 1:
                                    pool.wait_ge(pos_kept, g + 1)
                                if not first:
                                    pool.wait_ge(j_turned, g - 1)
                                    if one:
                                        pool.wait_ge(i_turned, g - 1)
                                    pool.nop(nofuse=True)
                                cols = gat_dst if one else gat_pos
                                ins = nc.gpsimd.tensor_copy(idx[:, b, 0, :], cols[:, bass.ds(G * g, G)])
                                if one:
                                    ins = nc.gpsimd.tensor_copy(idx[:, b, 1, :], gat_src[:, bass.ds(G * g, G)])
                                ins.then_inc(idx_ready, 1)
                                pool.wait_ge(idx_ready, g + 1)
                                pool.nop(nofuse=True)
                                from_ = x if one else agg_rows[layer - 1]
                                for j in range(G):
                                    nc.gpsimd.indirect_dma_start(fresh[:, b, j, :], None, from_[:, :],
                                                                 bass.IndirectOffsetOnAxis(ap=idx[:, b, 0, j:j + 1], axis=0)).then_inc(j_in[b], 16)
                                if one:
                                    for j in range(G):
                                        nc.gpsimd.indirect_dma_start(own[:, b, j, :], None, x[:, :],
                                                                     bass.IndirectOffsetOnAxis(ap=idx[:, b, 1, j:j + 1], axis=0)).then_inc(i_in[b], 16)
                        if layer == 1:
                            gather(0, True, False)
                            for i in range(LEAD - IN_LAYER_1, LEAD):
                                look_up(i)
                            with pool.Fori(1, STEPS - LEAD + 1) as i:
                                gather(i, False, False)
                                look_up(i + LEAD - 1)
                            for b in range(2):
                                keep(STEPS - 1, b)
                            with pool.Fori(STEPS - LEAD + 1, STEPS) as i:
                                gather(i, False, False)
                        else:
                            loop(pool, STEPS, gather)
                        if one and more:
                            for i in range(IN_MASKS, LEAD - IN_LAYER_1):
                                look_up(i)

                    @block.sync
                    def _(sp):
                        sp.dma_start(w_raw[:, 0, :, :], thetas[layer].rearrange("(m o) i -> o m i", o=P)).then_inc(w_in, 16)
                        sp.dma_start(w_raw[:, 1, :, :], phis[layer].rearrange("(m o) i -> o m i", o=P)).then_inc(w_in, 16)

                        def load_pen(g, b):
                            sp.dma_start(pen[:, b, :], end_row[bass.ds(g * GE, GE)].unsqueeze(0)).then_inc(pen_in[b], 16)

                        def load_own(g, b):
                            if not one:
                                sp.dma_start(own[:, b, :, :].rearrange("p a d -> p (a d)"),
                                             agg_cols[layer - 1][bass.ds(g, 1), :, :].rearrange("a p f -> p (a f)")).then_inc(i_in[b], 16)

                        for b in range(2):
                            load_own(b, b)
                            load_pen(b, b)

                        def store_rows(g, b):
                            sp.wait_ge(row_ready, g + 1)
                            sp.dma_start(agg_rows[layer][bass.ds(g * GE, GE), :].rearrange("(a p) d -> p a d", p=P), rows[:, b, :, :]).then_inc(row_out[b], 16)

                        def store_cols(g, b):
                            sp.wait_ge(agg_ready, 2 * g + 2)
                            sp.dma_start(agg_cols[layer][bass.ds(g, 1), :, :].rearrange("a p f -> p (a f)"),
                                         agg[:, b, :, :].rearrange("p k f -> p (k f)")).then_inc(agg_out[b], 16)

                        def step(i, first, last):
                            for b in range(2):
                                g = 2 * i + b
                                if not last:
                                    if not one:
                                        sp.wait_ge(i_full, g + 1)
                                        load_own(g + 2, b)
                                    sp.wait_ge(yz_ready, 2 * g + 2)
                                    load_pen(g + 2, b)
                                if not (first and b == 0):
                                    store_cols(g - 1, 1 - b)
                                    if more and not first:
                                        store_rows(g - 2, b)
                        loop(sp, STEPS, step)
                        store_cols(NG - 1, 1)
                        if more:
                            for b in range(2):
                                store_rows(NG - 2 + b, b)
                        for b in range(2):
                            if more:
                                sp.wait_ge(row_out[b], 16 * STEPS)
                            sp.wait_ge(agg_out[b], 16 * STEPS)

                    @block.tensor
                    def _(pe):
                        pe.wait_ge(w_in, 32 * (layer + 1))
                        for s in range(2):
                            if s == 1:
                                pe.wait_ge(w_ev, 4 * layer + 1)
                            for m in range(KD):
                                for k in range(KD):
                                    ins = nc.tensor.transpose(xt_ps[:, k, m * P:(m + 1) * P], w_raw[:, s, m, k * P:(k + 1) * P], ident[:])
                            ins.then_inc(w_t, 1)

                        def turn(rows_, b, signal):
                            for j in range(G):
                                for k in range(KD):
                                    ins = nc.tensor.transpose(xt_ps[:, k, j * P:(j + 1) * P], rows_[:, b, j, k * P:(k + 1) * P], ident[:])
                            ins.then_inc(signal, 1)

                        def turn_j(g, i, b, start):
                            pe.wait_ge(j_in[b], 64 * i + 64)
                            if start:
                                pe.wait_ge(w_ev, 4 * layer + 4)
                            else:
                                pe.wait_ge(i_ready if one else j_full, g)
                            turn(fresh, b, j_turned)

                        def turn_i(g, i, b):
                            pe.wait_ge(i_in[b], 64 * i + 64)
                            pe.wait_ge(j_ready, g + 1)
                            turn(own, b, i_turned)

                        def products(g, i, b, start):
                            pe.wait_ge(j_ready, g + 1)
                            pe.wait_ge(i_ready, g + 1)
                            pe.wait_ge(pen_in[b], 16 * i + 16)
                            for m in range(KD):
                                if not start:
                                    pe.wait_ge(sum_ready, 2 * g - 1 + m)
                                for s, to in enumerate((y_ps[m], z_ps[m])):
                                    for k in range(KD):
                                        out_m = slice(m * P, (m + 1) * P)
                                        nc.tensor.matmul(to[:, :], w_high[:, s, k, out_m], x_high[:, b, s, k, :], start=(k == 0), stop=False)
                                        nc.tensor.matmul(to[:, :], w_high[:, s, k, out_m], x_low[:, b, s, k, :], start=False, stop=False)
                                        nc.tensor.matmul(to[:, :], w_low[:, s, k, out_m], x_high[:, b, s, k, :], start=False,
                                                         stop=(s == 0 and k == KD - 1))
                                nc.tensor.matmul(z_ps[m][:, :], ones_bf[0:1, :], pen[:, b, :], start=False, stop=True).then_inc(yz_ready, 1)

                        def turn_back(g, b, start):
                            pe.wait_ge(agg_ready, 2 * g + 2)
                            if not start:
                                pe.wait_ge(row_ready, g)
                            for j in range(G):
                                for k in range(KD):
                                    ins = nc.tensor.transpose(row_ps[:, j, k * P:(k + 1) * P], agg[:, b, k, j * P:(j + 1) * P], ident[:])
                            ins.then_inc(row_turned, 1)

                        for b in range(2):
                            turn_j(b, 0, b, b == 0)
                            if one:
                                turn_i(b, 0, b)

                        def step(i, first, last):
                            for b in range(2):
                                g = 2 * i + b
                                start = first and b == 0
                                products(g, i, b, start)
                                if not last:
                                    turn_j(g + 2, i + 1, b, False)
                                if more and not start:
                                    turn_back(g - 1, 1 - b, first and b == 1)
                                if not last and one:
                                    turn_i(g + 2, i + 1, b)
                        loop(pe, STEPS, step)
                        if more:
                            turn_back(NG - 1, 1, False)

                    @block.scalar
                    def _(act):
                        def columns(g, i, b, start2):
                            act.wait_ge(j_turned, g + 1)
                            if not start2:
                                act.wait_ge(yz_ready, 2 * g - 2)
                            if one:
                                nc.scalar.copy(x_high[:, b, 0, :, :], xt_ps[:, :, :]).then_inc(j_high, 1)
                                act.wait_ge(i_turned, g + 1)
                                nc.scalar.copy(x_high[:, b, 1, :, :], xt_ps[:, :, :]).then_inc(i_high, 1)
                                return
                            for k in range(KD):
                                ins = nc.scalar.activation(x_full[:, b, 0, k, :], xt_ps[:, k, :], ACT.Relu, bias=bn_b[:, k:k + 1], scale=bn_a[:, k:k + 1])
                            ins.then_inc(j_full, 1)
                            act.wait_ge(i_in[b], 16 * i + 16)
                            own_k = own[:, b, :, :].rearrange("p a d -> p (a d)")
                            for k in range(KD):
                                ins = nc.scalar.activation(x_full[:, b, 1, k, :], own_k[:, k * GE:(k + 1) * GE], ACT.Relu, bias=bn_b[:, k:k + 1], scale=bn_a[:, k:k + 1])
                            ins.then_inc(i_full, 1)
                            act.wait_ge(j_full, g + 1)
                            nc.scalar.copy(x_high[:, b, 0, :, :], x_full[:, b, 0, :, :]).then_inc(j_high, 1)
                            act.wait_ge(i_full, g + 1)
                            nc.scalar.copy(x_high[:, b, 1, :, :], x_full[:, b, 1, :, :]).then_inc(i_high, 1)

                        for b in range(2):
                            columns(b, 0, b, True)

                        def step(i, first, last):
                            for b in range(2):
                                g = 2 * i + b
                                if not last:
                                    columns(g + 2, i + 1, b, False)
                                for m in range(KD):
                                    act.wait_ge(sum_ready, 2 * g + m + 1)
                                    if not first and m == 0:
                                        if more:
                                            act.wait_ge(row_turned, g - 1)
                                        act.wait_ge(agg_out[b], 16 * i)
                                    nc.scalar.activation(agg[:, b, m, :], summ[:, b, m, :], ACT.Relu,
                                                         accum_out=sums[:, 0, m, bass.ds(g, 1)]).then_inc(agg_ready, 1)
                                    act.wait_ge(agg_ready, 2 * g + m + 1)
                                    nc.scalar.activation(sq[:], agg[:, b, m, :], ACT.Square,
                                                         accum_out=sums[:, 1, m, bass.ds(g, 1)]).then_inc(sq_ready, 1)
                        loop(act, STEPS, step)
                        act.wait_ge(var_ready, layer + 1)
                        nc.scalar.activation(stat[:, 3, :], stat[:, 2, :], ACT.Sqrt).then_inc(sd_ready, 1)

                    @block.vector
                    def _(dve):
                        dve.wait_ge(w_t, 2 * layer + 1)
                        nc.vector.tensor_copy(w_full[:, 0, :, :], xt_ps[:, :, 0:D]).then_inc(w_ev, 1)
                        for b in range(2):
                            for m in range(KD):
                                nc.vector.memset(top[:, b, m, GE - 1:GE], 0.0)
                        dve.wait_ge(w_t, 2 * layer + 2)
                        dve.wait_ge(w_ev, 4 * layer + 1)
                        nc.vector.tensor_tensor(w_full[:, 1, :, :], xt_ps[:, :, 0:D], w_full[:, 0, :, :], ALU.subtract).then_inc(w_ev, 1)
                        dve.wait_ge(w_ev, 4 * layer + 2)
                        nc.vector.tensor_copy(w_high[:], w_full[:]).then_inc(w_ev, 1)
                        dve.wait_ge(w_ev, 4 * layer + 3)
                        nc.vector.tensor_tensor(w_low[:], w_full[:], w_high[:].bitcast(f32), ALU.subtract).then_inc(w_ev, 1)

                        def lows(g, b, start2):
                            for s, (high, ready) in enumerate(((j_high, j_ready), (i_high, i_ready))):
                                dve.wait_ge(high, g + 1)
                                if not start2 and s == 0:
                                    dve.wait_ge(yz_ready, 2 * g - 2)
                                full = xt_ps[:, :, :] if one else x_full[:, b, s, :, :]
                                nc.vector.tensor_tensor(x_low[:, b, s, :, :], full, x_high[:, b, s, :, :].bitcast(f32), ALU.subtract).then_inc(ready, 1)

                        for b in range(2 if one else 1):
                            lows(b, b, True)
                        chain = Chain(dve, s_dve)

                        def step(i, first, last):
                            chain.step(i)
                            for b in range(2):
                                g = 2 * i + b
                                for m in range(KD):
                                    dve.wait_ge(yz_ready, 2 * g + m + 1)
                                    chain.mark(nc.vector.tensor_tensor_scan(top[:, b, m, :], mask[:, bass.ds(g * GE, GE)], y_ps[m][:, :],
                                                                            top[:, 1 - b, m, GE - 1:GE], ALU.add, ALU.max))
                                    if not first:
                                        dve.wait_ge(agg_ready, 2 * g - 3 + m)
                                    chain.after()
                                    nc.vector.tensor_tensor(summ[:, b, m, :], z_ps[m][:, :], top[:, b, m, :], ALU.add).then_inc(sum_ready, 1)
                                    if not one and m == 0 and not (last and b == 1):
                                        lows(g + 1, 1 - b, first and b == 0)
                                if one and not last:
                                    lows(g + 2, b, False)
                                if more and b == 1:
                                    dve.wait_ge(row_turned, g)
                                    if not first:
                                        dve.wait_ge(row_out[0], 16 * i)
                                    nc.vector.tensor_copy(rows[:, 0, :, :], row_ps[:, :, :]).then_inc(row_ready, 1)
                                elif more and not first:
                                    dve.wait_ge(row_turned, g)
                                    if not (isinstance(i, int) and i < 2):
                                        dve.wait_ge(row_out[1], 16 * (i - 1))
                                    nc.vector.tensor_copy(rows[:, 1, :, :], row_ps[:, :, :]).then_inc(row_ready, 1)
                        loop(dve, STEPS, step, peeled=2)
                        if more:
                            dve.wait_ge(row_turned, NG)
                            dve.wait_ge(row_out[1], 16 * (STEPS - 1))
                            nc.vector.tensor_copy(rows[:, 1, :, :], row_ps[:, :, :]).then_inc(row_ready, 1)

                        dve.wait_ge(sq_ready, 2 * NG)
                        base_count = chain.base + chain.count
                        n = [base_count]

                        def link(ins):
                            n[0] += 1
                            ins.then_inc(s_dve, 1)
                            dve.wait_ge(s_dve, n[0])

                        for s in range(2):
                            link(nc.vector.tensor_reduce(stat[:, s, :], sums[:, s, :, :], AX_X, ALU.add))
                        link(nc.vector.tensor_scalar(stat[:, 0:2, :], stat[:, 0:2, :], 1.0 / N, None, ALU.mult))
                        link(nc.vector.tensor_tensor(stat[:, 2, :], stat[:, 0, :], stat[:, 0, :], ALU.mult))
                        link(nc.vector.tensor_tensor(stat[:, 2, :], stat[:, 1, :], stat[:, 2, :], ALU.subtract))
                        nc.vector.tensor_scalar(stat[:, 2, :], stat[:, 2, :], 0.0, EPS, ALU.max, ALU.add).then_inc(var_ready, 1)
                        dve.wait_ge(sd_ready, layer + 1)
                        link(nc.vector.reciprocal(stat[:, 4, :], stat[:, 3, :]))
                        link(nc.vector.tensor_tensor(bn_a[:], stat[:, 4, :], gam[:, :, layer], ALU.mult))
                        link(nc.vector.tensor_tensor(stat[:, 5, :], stat[:, 0, :], bn_a[:], ALU.mult))
                        nc.vector.tensor_tensor(bn_b[:], bet[:, :, layer], stat[:, 5, :], ALU.subtract)

        layering.close()

        with ExitStack() as ctx:
            spread = sb("spread", [P, KD, P], f32, ctx)
            base_row = sb("base_row", [P, 2, D], f32, ctx)
            base_part = sb("base_part", [P, 3, 2, D], bf16, ctx)
            base_left = sb("base_left", [P, 2, 2, D], f32, ctx)
            base3 = sb("base3", [P, 2, D], bf16, ctx)
            xin = sb("xin", [P, 4, R, D], f32, ctx)
            xout = sb("xout", [P, 4, R, D], f32, ctx)
            own = sb("own_f", [P, 2, KD, GE], f32, ctx)
            act_cols = sb("act_cols", [P, 2, KD, GE], f32, ctx)
            xs = sb("xs", [P, 2, G, D], f32, ctx)
            yf = sb("yf", [P, 2, G, D], f32, ctx)
            idx = sb("idx_f", [P, 2, G], i32, ctx)
            work = {}
            for kind, rows_ in (("b", R), ("f", G)):
                work[kind] = (sb("bstats" + kind, [P, 2, rows_, 6], f32, ctx), sb("aggr" + kind, [P, 2, rows_, 2], f32, ctx),
                              sb("sd" + kind, [P, 2, rows_], f32, ctx), sb("rstd" + kind, [P, 2, rows_], f32, ctx),
                              sb("shift" + kind, [P, 2, rows_], f32, ctx))
            sum_ps = [pb(f"sum_ps{s}", [P, R, D], f32, ctx) for s in range(2)]
            fin_ps = pb("fin_ps", [P, G, D], f32, ctx)
            names = ("spread_ready", "spread_turned", "base_ready", "s_dve", "added_b", "added_f", "aggr_b", "aggr_f", "sd_b", "sd_f",
                     "norm_b", "norm_f", "y_b", "y_f", "act_ready", "idx_ready")
            (spread_ready, spread_turned, base_ready, s_dve, added_b, added_f, aggr_b, aggr_f, sd_b, sd_f,
             norm_b, norm_f, y_b, y_f, act_ready, idx_ready) = [whole.enter_context(nc.semaphore(n + "_o")) for n in names]
            x_in, out_done = [[whole.enter_context(nc.semaphore(f"{n}{k}")) for k in range(4)] for n in ("x_in", "out_done")]
            own_in, xs_in, done_out = [[whole.enter_context(nc.semaphore(f"{n}{b}_o")) for b in range(2)]
                                       for n in ("own_in", "xs_in", "done_out")]
            x_blocks = x[0:BLOCKS * BLOCK_ROWS, :].rearrange("(n p r) d -> n p (r d)", p=P, r=R)
            out_blocks = out[0:BLOCKS * BLOCK_ROWS, :].rearrange("(n p r) d -> n p (r d)", p=P, r=R)
            tail = [(P, R)] * (BLOCKS - 4 * BLOCK_STEPS) + ([(REST // RR, RR)] if REST else [])

            def stages(engine, step, tail_step, edges_over=lambda: None):
                step(0, True, False, True, True)
                with engine.Fori(1, STEPS - 1) as i:
                    step(i, False, False, True, True)
                step(STEPS - 1, False, False, True, False)
                edges_over()
                if BLOCK_STEPS - 1 > STEPS:
                    with engine.Fori(STEPS, BLOCK_STEPS - 1) as i:
                        step(i, False, False, False, False)
                step(BLOCK_STEPS - 1, False, True, False, False)
                for k in range(len(tail)):
                    tail_step(k)

            with nc.Block() as block:
                @block.sync
                def _(sp):
                    def load(i, k, np_=P, r_=R):
                        if np_ == P and r_ == R:
                            from_ = x_blocks[bass.ds(4 * i + k, 1), :, :].rearrange("a p f -> p (a f)")
                        else:
                            from_ = x[N - REST:N, :].rearrange("(p r) d -> p (r d)", r=RR)
                        sp.dma_start(xin[0:np_, k, 0:r_, :].rearrange("p r d -> p (r d)"), from_).then_inc(x_in[k], 16)

                    def load_own(g, b):
                        sp.dma_start(own[:, b, :, :].rearrange("p k f -> p (k f)"),
                                     agg_cols[LAYERS - 1][bass.ds(g, 1), :, :].rearrange("a p f -> p (a f)")).then_inc(own_in[b], 16)

                    def store(i, k, np_=P, r_=R):
                        sp.wait_ge(y_b, PAIRS * (4 * i + k + 1))
                        if np_ == P and r_ == R:
                            to = out_blocks[bass.ds(4 * i + k, 1), :, :].rearrange("a p f -> p (a f)")
                        else:
                            to = out[N - REST:N, :].rearrange("(p r) d -> p (r d)", r=RR)
                        sp.dma_start(to, xout[0:np_, k, 0:r_, :].rearrange("p r d -> p (r d)")).then_inc(out_done[k], 16)

                    for b in range(2):
                        load_own(b, b)
                    for k in range(4):
                        load(0, k)

                    def store_group(g, b):
                        sp.wait_ge(y_f, g + 1)
                        sp.dma_start(done_rows[bass.ds(g * GE, GE), :].rearrange("(a p) d -> p a d", p=P), yf[:, b, :, :]).then_inc(done_out[b], 16)

                    def step(i, first, last, edges, ahead):
                        for k in range(4):
                            b = k // 2
                            g = 2 * i + b
                            if not last or k < len(tail):
                                sp.wait_ge(added_b, PAIRS * (4 * i + k + 1))
                                load(i + 1, k, *(tail[k] if last else ()))
                            if k % 2 and ahead:
                                sp.wait_ge(act_ready, g + 1)
                                load_own(g + 2, b)
                            if k or not first:
                                store(i if k else i - 1, (k - 1) % 4)
                            if k % 2 == 0 and edges and (k or not first):
                                store_group(g - 1, 1 - b)
                        if last:
                            store(i, 3)
                    stages(sp, step, lambda k: store(BLOCK_STEPS, k, *tail[k]), lambda: store_group(NG - 1, 1))
                    for k in range(4):
                        sp.wait_ge(out_done[k], 16 * (BLOCK_STEPS + (k < len(tail))))
                    for b in range(2):
                        sp.wait_ge(done_out[b], 16 * STEPS)

                @block.gpsimd
                def _(pool):
                    def step(i, first, last):
                        for b in range(2):
                            g = 2 * i + b
                            if not first:
                                pool.wait_ge(added_f, g - 1)
                                pool.nop(nofuse=True)
                            nc.gpsimd.tensor_copy(idx[:, b, :], gat_src[:, bass.ds(G * g, G)]).then_inc(idx_ready, 1)
                            pool.wait_ge(idx_ready, g + 1)
                            pool.nop(nofuse=True)
                            for j in range(G):
                                nc.gpsimd.indirect_dma_start(xs[:, b, j, :], None, x[:, :],
                                                             bass.IndirectOffsetOnAxis(ap=idx[:, b, j:j + 1], axis=0)).then_inc(xs_in[b], 16)
                    loop(pool, STEPS, step)

                @block.tensor
                def _(pe):
                    pe.wait_ge(spread_ready, 1)
                    for k in range(KD):
                        ins = nc.tensor.matmul(fin_ps[:, 0, k * P:(k + 1) * P], spread[:, k, :], ident[:], start=True, stop=True)
                    ins.then_inc(spread_turned, 1)
                    pe.wait_ge(base_ready, 1)

                    def add_block(i, k, np_, r_, start):
                        n = 4 * i + k
                        pe.wait_ge(x_in[k], 16 * i + 16)
                        for q in range(0, r_, 2):
                            if not start:
                                pe.wait_ge(y_b, PAIRS * (n - 2) + q // 2 + 1)
                            to = sum_ps[k % 2][0:np_, q:q + 2, :].rearrange("p r d -> p (r d)")
                            nc.tensor.matmul(to, ident[0:np_, 0:np_], xin[0:np_, k, q:q + 2, :].rearrange("p r d -> p (r d)"), start=True, stop=False)
                            ins = nc.tensor.matmul(to, ones_bf[0:3, 0:np_], base3[0:3, :, :].rearrange("p r d -> p (r d)"), start=False, stop=True)
                            ins.then_inc(added_b, 1 if q + 2 < r_ else PAIRS - q // 2)

                    def add_group(i, b, start):
                        g = 2 * i + b
                        pe.wait_ge(xs_in[b], 64 * i + 64)
                        pe.wait_ge(act_ready, g + 1)
                        if not start:
                            pe.wait_ge(y_f, g)
                        for q in range(0, G, 2):
                            nc.tensor.matmul(fin_ps[:, q:q + 2, :].rearrange("p r d -> p (r d)"), ident[:],
                                             xs[:, b, q:q + 2, :].rearrange("p r d -> p (r d)"), start=True, stop=False)
                            for j in (q, q + 1):
                                for k in range(KD):
                                    ins = nc.tensor.matmul(fin_ps[:, j, k * P:(k + 1) * P], act_cols[:, b, k, j * P:(j + 1) * P], ident[:],
                                                           start=False, stop=(j == q + 1 and k == KD - 1))
                        ins.then_inc(added_f, 1)

                    def step(i, first, last, edges, ahead):
                        for k in range(4):
                            add_block(i, k, P, R, first and k < 2)
                            if k % 2 and edges:
                                add_group(i, k // 2, first and k == 1)
                    stages(pe, step, lambda k: add_block(BLOCK_STEPS, k, *tail[k], False))

                @block.vector
                def _(dve):
                    chain = Chain(dve, s_dve)

                    def link(ins):
                        chain.mark(ins)
                        chain.after()

                    for k in range(KD):
                        ins = nc.vector.tensor_scalar(spread[:, k, :], ones[:], bn_b[:, k:k + 1], None, ALU.mult)
                    ins.then_inc(spread_ready, 1)
                    dve.wait_ge(spread_turned, 1)
                    for r in range(2):
                        link(nc.vector.tensor_scalar(base_row[:, r, :], fin_ps[:, 0, :], 0.0, None, ALU.max))
                    link(nc.vector.tensor_copy(base_part[:, 0, :, :], base_row[:]))
                    link(nc.vector.tensor_tensor(base_left[:, 0, :, :], base_row[:], base_part[:, 0, :, :], ALU.subtract))
                    link(nc.vector.tensor_copy(base_part[:, 1, :, :], base_left[:, 0, :, :]))
                    link(nc.vector.tensor_tensor(base_left[:, 1, :, :], base_left[:, 0, :, :], base_part[:, 1, :, :], ALU.subtract))
                    link(nc.vector.tensor_copy(base_part[:, 2, :, :], base_left[:, 1, :, :]))
                    link(nc.vector.tensor_scalar(base3[:], base_part[:, 0, :, :], ident[:, 0:1], None, ALU.mult))
                    link(nc.vector.scalar_tensor_tensor(base3[:], base_part[:, 1, :, :], ident[:, 1:2], base3[:], ALU.mult, ALU.add))
                    nc.vector.scalar_tensor_tensor(base3[:], base_part[:, 2, :, :], ident[:, 2:3], base3[:], ALU.mult, ALU.add).then_inc(base_ready, 1)
                    set_up = chain.count

                    def factors(kind, n, s, ps, aggr_, sd_, y_, norm_, np_, r_, base):
                        bstats, aggr, sd, rstd, shift = work[kind]
                        for r in range(r_):
                            if kind == "f" and r == 0:
                                dve.wait_ge(added_f, n + 1)
                            elif kind == "b" and r % 2 == 0:
                                dve.wait_ge(added_b, PAIRS * n + r // 2 + 1)
                            ins = nc.vector.bn_stats(bstats[0:np_, s, r, :], ps[0:np_, r, :])
                        chain.mark(ins)
                        chain.after()
                        dve.nop(nofuse=True)
                        for r in range(r_):
                            ins = nc.vector.bn_aggr(aggr[0:np_, s, r, :], bstats[0:np_, s, r, :])
                        chain.mark(ins)
                        chain.after()
                        nc.vector.tensor_scalar(sd[0:np_, s, 0:r_], aggr[0:np_, s, 0:r_, 1], EPS, None, ALU.add).then_inc(aggr_, 1)
                        dve.wait_ge(sd_, n + 1)
                        if base:
                            dve.wait_ge(y_, PAIRS * (n - 1) if kind == "b" else n - 1)
                        chain.mark(nc.vector.reciprocal(rstd[0:np_, s, 0:r_], sd[0:np_, s, 0:r_]))
                        chain.after()
                        nc.vector.scalar_tensor_tensor(shift[0:np_, s, 0:r_], aggr[0:np_, s, 0:r_, 0], -1.0, rstd[0:np_, s, 0:r_],
                                                       ALU.mult, ALU.mult).then_inc(norm_, 1)

                    def of_block(i, k, np_, r_, start):
                        factors("b", 4 * i + k, k % 2, sum_ps[k % 2], aggr_b, sd_b, y_b, norm_b, np_, r_, not start)

                    def of_group(i, b, start):
                        factors("f", 2 * i + b, b, fin_ps, aggr_f, sd_f, y_f, norm_f, P, G, not start)

                    MARKS = 3

                    def step(i, first, last, edges, ahead):
                        chain.base = set_up + MARKS * (6 * i if edges else 6 * STEPS + 4 * (i - STEPS))
                        chain.count = 0
                        for k in range(4):
                            of_block(i, k, P, R, first and k < 2)
                            if k % 2 and edges:
                                of_group(i, k // 2, first)

                    def tail_step(k):
                        chain.base, chain.count = set_up + MARKS * (6 * STEPS + 4 * (BLOCK_STEPS - STEPS) + k), 0
                        of_block(BLOCK_STEPS, k, *tail[k], False)
                    stages(dve, step, tail_step)

                @block.scalar
                def _(act):
                    def normalise(kind, n, s, ps, to, aggr_, sd_, norm_, np_, r_, freed):
                        _, _, sd, rstd, shift = work[kind]
                        act.wait_ge(aggr_, n + 1)
                        nc.scalar.activation(sd[0:np_, s, 0:r_], sd[0:np_, s, 0:r_], ACT.Sqrt).then_inc(sd_, 1)
                        if freed:
                            act.wait_ge(*freed)
                        act.wait_ge(norm_, n + 1)
                        for r in range(r_):
                            ins = nc.scalar.activation(to[0:np_, r, :], ps[0:np_, r, :], ACT.Identity,
                                                       bias=shift[0:np_, s, r:r + 1], scale=rstd[0:np_, s, r:r + 1])
                            if kind == "b" and r % 2:
                                ins.then_inc(y_b, 1 if r + 1 < r_ else PAIRS - r // 2)
                        if kind == "f":
                            ins.then_inc(y_f, 1)

                    def activate(g, i, b):
                        act.wait_ge(own_in[b], 16 * i + 16)
                        for k in range(KD):
                            ins = nc.scalar.activation(act_cols[:, b, k, :], own[:, b, k, :], ACT.Relu, bias=bn_b[:, k:k + 1], scale=bn_a[:, k:k + 1])
                        ins.then_inc(act_ready, 1)

                    for b in range(2):
                        activate(b, 0, b)

                    def of_block(i, k, np_, r_):
                        n = 4 * i + k
                        freed = None if isinstance(i, int) and i == 0 else (out_done[k], 16 * i)
                        normalise("b", n, k % 2, sum_ps[k % 2], xout[:, k, :, :], aggr_b, sd_b, norm_b, np_, r_, freed)

                    def step(i, first, last, edges, ahead):
                        for k in range(4):
                            of_block(i, k, P, R)
                            if k % 2 and edges:
                                b = k // 2
                                g = 2 * i + b
                                normalise("f", g, b, fin_ps, yf[:, b, :, :], aggr_f, sd_f, norm_f, P, G, None if first else (done_out[b], 16 * i))
                                if ahead:
                                    activate(g + 2, i + 1, b)
                    stages(act, step, lambda k: of_block(BLOCK_STEPS, k, *tail[k]))

        with ExitStack() as ctx:
            SLOTS = max(n for n in range(2, 6) if NG % n == 0)
            yo = sb("yo", [P, SLOTS, G, D], f32, ctx)
            idx = sb("idx_p", [P, SLOTS, G], i32, ctx)
            idx_ready = whole.enter_context(nc.semaphore("idx_ready_p"))
            yo_in, put = [[whole.enter_context(nc.semaphore(f"{n}{b}_p")) for b in range(SLOTS)] for n in ("yo_in", "put")]
            with nc.Block() as block:
                @block.sync
                def _(sp):
                    def step(i, first, last):
                        for b in range(SLOTS):
                            g = SLOTS * i + b
                            if not first:
                                sp.wait_ge(put[b], 64 * i)
                                sp.nop(nofuse=True)
                                sp.wait_ge(yo_in[b], 16 * i)
                            sp.dma_start(yo[:, b, :, :], done_rows[bass.ds(g * GE, GE), :].rearrange("(a p) d -> p a d", p=P)).then_inc(yo_in[b], 16)
                    loop(sp, NG // SLOTS, step)

                @block.gpsimd
                def _(pool):
                    def step(i, first, last):
                        for b in range(SLOTS):
                            g = SLOTS * i + b
                            if not first:
                                pool.wait_ge(put[b], 64 * i)
                                pool.nop(nofuse=True)
                            nc.gpsimd.tensor_copy(idx[:, b, :], put_src[:, bass.ds(G * g, G)]).then_inc(idx_ready, 1)
                            pool.wait_ge(idx_ready, g + 1)
                            pool.wait_ge(yo_in[b], 16 * i + 16)
                            pool.nop(nofuse=True)
                            for j in range(G):
                                nc.gpsimd.indirect_dma_start(out[:, :], bass.IndirectOffsetOnAxis(ap=idx[:, b, j:j + 1], axis=0),
                                                             yo[:, b, j, :], None, bounds_check=N - 1, oob_is_err=False).then_inc(put[b], 16)
                    loop(pool, NG // SLOTS, step)
                    for b in range(SLOTS):
                        pool.wait_ge(put[b], 64 * (NG // SLOTS))
                        pool.nop(nofuse=True)


_INS = ['x', 'src', 'dst', 'L0_gnn_thetas', 'L0_gnn_phis', 'L0_gnn_gammas', 'L0_gnn_betas']


def kernel(**inputs):
    import numpy as _np
    import concourse.bacc as _bacc
    from concourse import mybir as _mybir
    from concourse.bass_utils import run_bass_kernel_spmd as _run

    nc = _bacc.Bacc("TRN2", target_bir_lowering=False, num_devices=1)
    arrays, args = {}, []
    for name in _INS:
        a = _np.ascontiguousarray(inputs[name])
        arrays[f"in_{name}_dram"] = a
        args.append(nc.dram_tensor(f"in_{name}_dram", a.shape, _mybir.dt.from_np(a.dtype), kind="ExternalInput").ap())
    args.append(nc.dram_tensor("out_0_dram", inputs['x'].shape, _mybir.dt.float32, kind="ExternalOutput").ap())
    gnn_program(nc, *args)
    r = _run(nc, [arrays], core_ids=[0])
    return r.results[0]["out_0_dram"]
```
